# Optimizing a Trainium2 kernel written in Bass

```python
import numpy as np
import jax
import jax.numpy as jnp

def _softmax(x, axis=-1):
    return jax.nn.softmax(x, axis=axis)

def _gelu(x):
    return jax.nn.gelu(x, approximate=True)

def _silu(x):
    return jax.nn.silu(x)

def _sigmoid(x):
    return jax.nn.sigmoid(x)

def _layernorm(x, axis=-1, eps=1e-05):
    m = jnp.mean(x, axis=axis, keepdims=True)
    v = jnp.var(x, axis=axis, keepdims=True)
    return (x - m) / jnp.sqrt(v + eps)

def _scatter_add(tgt, idx, src, axis=0):
    return tgt.at[idx].add(src)

def _segment_sum(src, seg, n):
    return jax.ops.segment_sum(src, seg, n)
kernel_name = 'mk_gnn_preln_d4_gnn_r8_de6686'

def setup_inputs(seed: int=0):
    np.random.seed(seed)
    _w = jnp.asarray

    def _rec_inputs():
        import jax
        import jax.numpy as jnp
        _gk = jax.random.key(seed)
        x = -0.000202 + 1 * jax.random.normal(jax.random.fold_in(_gk, 1), (6250, 128), jnp.float32)
        src = jax.random.randint(jax.random.fold_in(_gk, 2), (100000,), 0, 6250, jnp.int32)
        dst = jax.random.randint(jax.random.fold_in(_gk, 3), (100000,), 0, 6250, jnp.int32)
        _o = jnp.argsort(dst, stable=True)
        src = src[_o]
        dst = dst[_o]
        edge_weight = jax.random.uniform(jax.random.fold_in(_gk, 13), (100000,), jnp.float32, 0.0, 1)
        return (x, src, dst, edge_weight)
    x, src, dst, edge_weight = _rec_inputs()

    def _L0_gnn_setup():
        import jax, jax.numpy as jnp
        import numpy as np
        N = 6250
        E = 200000
        D = 128
        L = 3
        key = jax.random.key(seed)
        ks = jax.random.split(key, 8)
        x = jax.random.normal(ks[0], (N, D), dtype=jnp.float32)
        edge_index = jax.random.randint(ks[1], (2, E), 0, N, dtype=jnp.int64)
        s = 1.0 / np.sqrt(D)
        W_pre = jax.random.uniform(ks[2], (D, D), jnp.float32, -s, s)
        b_pre = jnp.zeros((D,), jnp.float32)
        W_conv = jax.random.uniform(ks[3], (L, D, D), jnp.float32, -s, s)
        b_conv = jnp.zeros((L, D), jnp.float32)
        s2 = 1.0 / np.sqrt(2 * D)
        W_upd = jax.random.uniform(ks[4], (L, 2 * D, D), jnp.float32, -s2, s2)
        b_upd = jnp.zeros((L, D), jnp.float32)
        return {'x': x, 'edge_index': edge_index, 'W_pre': W_pre, 'b_pre': b_pre, 'W_conv': W_conv, 'b_conv': b_conv, 'W_upd': W_upd, 'b_upd': b_upd}
    _L0_gnn_all = _L0_gnn_setup()
    _L0_gnn_in = {k: v for k, v in _L0_gnn_all.items() if k in ('W_pre', 'b_pre', 'W_conv', 'b_conv', 'W_upd', 'b_upd')}
    del _L0_gnn_all

    def _L1_gnn_setup():
        import jax, jax.numpy as jnp
        import numpy as np
        N_NODES = 6250
        N_EDGES = 50000
        IN_DIM = 128
        HIDDEN = 128
        OUT_DIM = 128
        MIX = 4

        def _gelu(x):
            return jax.nn.gelu(x, approximate=False)
        key = jax.random.key(seed)
        ks = jax.random.split(key, 8)
        X = jax.random.normal(ks[0], (N_NODES, IN_DIM), dtype=jnp.float32)
        edge_index = jax.random.randint(ks[1], (2, N_EDGES), 0, N_NODES, dtype=jnp.int64)
        s = lambda fan_in: 1.0 / np.sqrt(fan_in)
        W1 = jax.random.uniform(ks[2], (HIDDEN, IN_DIM), jnp.float32, -s(IN_DIM), s(IN_DIM))
        b1 = jax.random.uniform(ks[3], (HIDDEN,), jnp.float32, -s(IN_DIM), s(IN_DIM))
        WA = jax.random.uniform(ks[4], (HIDDEN, HIDDEN), jnp.float32, -s(HIDDEN), s(HIDDEN))
        WB = jax.random.uniform(ks[5], (MIX, HIDDEN), jnp.float32, -s(HIDDEN), s(HIDDEN))
        W2 = jax.random.uniform(ks[6], (OUT_DIM, 2 * HIDDEN), jnp.float32, -s(2 * HIDDEN), s(2 * HIDDEN))
        b2 = jax.random.uniform(ks[7], (OUT_DIM,), jnp.float32, -s(2 * HIDDEN), s(2 * HIDDEN))
        return {'X': X, 'edge_index': edge_index, 'W1': W1, 'b1': b1, 'WA': WA, 'WB': WB, 'W2': W2, 'b2': b2}
    _L1_gnn_all = _L1_gnn_setup()
    _L1_gnn_in = {k: v for k, v in _L1_gnn_all.items() if k in ('W1', 'b1', 'WA', 'WB', 'W2', 'b2')}
    del _L1_gnn_all

    def _L2_gnn_setup():
        import jax, jax.numpy as jnp
        import numpy as np
        N = 12500
        E = 100000
        D = 128
        key = jax.random.key(seed)
        ks = jax.random.split(key, 12)
        s = lambda fan_in: 1.0 / np.sqrt(fan_in)
        return {'h': jax.random.normal(ks[0], (N, D), dtype=jnp.float32), 'w': jax.random.uniform(ks[1], (E,), dtype=jnp.float32), 'src': jax.random.randint(ks[2], (E,), 0, N, dtype=jnp.int32), 'dst': jax.random.randint(ks[3], (E,), 0, N, dtype=jnp.int32), 'W1': jax.random.uniform(ks[4], (2 * D + 1, D), jnp.float32, -s(2 * D + 1), s(2 * D + 1)), 'b1': jnp.zeros((D,), jnp.float32), 'W2': jax.random.uniform(ks[5], (D, D), jnp.float32, -s(D), s(D)), 'b2': jnp.zeros((D,), jnp.float32), 'U1': jax.random.uniform(ks[6], (2 * D, D), jnp.float32, -s(2 * D), s(2 * D)), 'c1': jnp.zeros((D,), jnp.float32), 'U2': jax.random.uniform(ks[7], (D, D), jnp.float32, -s(D), s(D)), 'c2': jnp.zeros((D,), jnp.float32)}
    _L2_gnn_all = _L2_gnn_setup()
    _L2_gnn_in = {k: v for k, v in _L2_gnn_all.items() if k in ('W1', 'b1', 'W2', 'b2', 'U1', 'c1', 'U2', 'c2')}
    del _L2_gnn_all

    def _L3_gnn_setup():
        import jax, jax.numpy as jnp
        import numpy as np
        N_NODES = 6250
        N_EDGES = 100000
        DIM = 128
        BN_EPS = 1e-05
        key = jax.random.key(seed)
        ks = jax.random.split(key, 12)
        d = DIM
        s = 1.0 / np.sqrt(d)
        x = jax.random.normal(ks[0], (N_NODES, d), dtype=jnp.float32)
        edge_index = jax.random.randint(ks[1], (2, N_EDGES), 0, N_NODES, dtype=jnp.int64)
        W_msg = jax.random.uniform(ks[2], (d, d), jnp.float32, -s, s)
        b_msg = jax.random.uniform(ks[3], (d,), jnp.float32, -s, s)
        sa = 1.0 / np.sqrt(2 * d)
        W_att = jax.random.uniform(ks[4], (2 * d, 1), jnp.float32, -sa, sa)
        b_att = jax.random.uniform(ks[5], (1,), jnp.float32, -sa, sa)
        W_ih = jax.random.uniform(ks[6], (3 * d, d), jnp.float32, -s, s)
        b_ih = jax.random.uniform(ks[7], (3 * d,), jnp.float32, -s, s)
        W_hh = jax.random.uniform(ks[8], (3 * d, d), jnp.float32, -s, s)
        b_hh = jax.random.uniform(ks[9], (3 * d,), jnp.float32, -s, s)
        gamma = jnp.ones((d,), jnp.float32)
        beta = jnp.zeros((d,), jnp.float32)
        return {'x': x, 'edge_index': edge_index, 'W_msg': W_msg, 'b_msg': b_msg, 'W_att': W_att, 'b_att': b_att, 'W_ih': W_ih, 'b_ih': b_ih, 'W_hh': W_hh, 'b_hh': b_hh, 'gamma': gamma, 'beta': beta}
    _L3_gnn_all = _L3_gnn_setup()
    _L3_gnn_in = {k: v for k, v in _L3_gnn_all.items() if k in ('W_msg', 'b_msg', 'W_att', 'b_att', 'W_ih', 'b_ih', 'W_hh', 'b_hh', 'gamma', 'beta')}
    del _L3_gnn_all
    return {'x': x, 'src': src, 'dst': dst, 'edge_weight': edge_weight, 'L0_gnn_W_pre': _L0_gnn_in['W_pre'], 'L0_gnn_b_pre': _L0_gnn_in['b_pre'], 'L0_gnn_W_conv': _L0_gnn_in['W_conv'], 'L0_gnn_b_conv': _L0_gnn_in['b_conv'], 'L0_gnn_W_upd': _L0_gnn_in['W_upd'], 'L0_gnn_b_upd': _L0_gnn_in['b_upd'], 'L1_gnn_W1': _L1_gnn_in['W1'], 'L1_gnn_b1': _L1_gnn_in['b1'], 'L1_gnn_WA': _L1_gnn_in['WA'], 'L1_gnn_WB': _L1_gnn_in['WB'], 'L1_gnn_W2': _L1_gnn_in['W2'], 'L1_gnn_b2': _L1_gnn_in['b2'], 'L2_gnn_W1': _L2_gnn_in['W1'], 'L2_gnn_b1': _L2_gnn_in['b1'], 'L2_gnn_W2': _L2_gnn_in['W2'], 'L2_gnn_b2': _L2_gnn_in['b2'], 'L2_gnn_U1': _L2_gnn_in['U1'], 'L2_gnn_c1': _L2_gnn_in['c1'], 'L2_gnn_U2': _L2_gnn_in['U2'], 'L2_gnn_c2': _L2_gnn_in['c2'], 'L3_gnn_W_msg': _L3_gnn_in['W_msg'], 'L3_gnn_b_msg': _L3_gnn_in['b_msg'], 'L3_gnn_W_att': _L3_gnn_in['W_att'], 'L3_gnn_b_att': _L3_gnn_in['b_att'], 'L3_gnn_W_ih': _L3_gnn_in['W_ih'], 'L3_gnn_b_ih': _L3_gnn_in['b_ih'], 'L3_gnn_W_hh': _L3_gnn_in['W_hh'], 'L3_gnn_b_hh': _L3_gnn_in['b_hh'], 'L3_gnn_gamma': _L3_gnn_in['gamma'], 'L3_gnn_beta': _L3_gnn_in['beta']}

def reference(x, src, dst, edge_weight, L0_gnn_W_pre, L0_gnn_b_pre, L0_gnn_W_conv, L0_gnn_b_conv, L0_gnn_W_upd, L0_gnn_b_upd, L1_gnn_W1, L1_gnn_b1, L1_gnn_WA, L1_gnn_WB, L1_gnn_W2, L1_gnn_b2, L2_gnn_W1, L2_gnn_b1, L2_gnn_W2, L2_gnn_b2, L2_gnn_U1, L2_gnn_c1, L2_gnn_U2, L2_gnn_c2, L3_gnn_W_msg, L3_gnn_b_msg, L3_gnn_W_att, L3_gnn_b_att, L3_gnn_W_ih, L3_gnn_b_ih, L3_gnn_W_hh, L3_gnn_b_hh, L3_gnn_gamma, L3_gnn_beta):
    import jax
    import jax.numpy as jnp

    def _L0_gnn_ref(x, edge_index, W_pre, b_pre, W_conv, b_conv, W_upd, b_upd):
        import jax, jax.numpy as jnp
        import numpy as np
        N = 6250
        E = 200000
        D = 128
        L = 3
        h = x @ W_pre + b_pre
        src = edge_index[0]
        dst = edge_index[1]
        loop_mask = (src != dst).astype(h.dtype)[:, None]
        for l in range(L):
            msgs = h[src] * loop_mask
            agg = jax.ops.segment_sum(msgs, dst, num_segments=N)
            x_neigh = agg @ W_conv[l] + b_conv[l]
            h = jnp.concatenate([x_neigh, h], axis=-1) @ W_upd[l] + b_upd[l]
            h = jax.nn.relu(h)
        return h

    def _L1_gnn_ref(X, edge_index, W1, b1, WA, WB, W2, b2):
        import jax, jax.numpy as jnp
        import numpy as np
        N_NODES = 6250
        N_EDGES = 50000
        IN_DIM = 128
        HIDDEN = 128
        OUT_DIM = 128
        MIX = 4

        def _gelu(x):
            return jax.nn.gelu(x, approximate=False)
        num_nodes = X.shape[0]
        H = _gelu(X @ W1.T + b1)
        src, dst = (edge_index[0], edge_index[1])
        X_src = H[src]
        W_tar = _gelu(X_src @ WA.T) @ WB.T
        cross = X_src[:, :, None] * W_tar[:, None, :]
        agg = jax.ops.segment_sum(cross, dst, num_segments=num_nodes)
        agg = _gelu(agg)
        out_edge = jnp.einsum('ehm,em->eh', agg[dst], W_tar)
        ones = jnp.ones((src.shape[0],), X.dtype)
        cnt = jax.ops.segment_sum(ones, dst, num_segments=num_nodes)
        agg_node = jax.ops.segment_sum(out_edge, dst, num_segments=num_nodes)
        agg_node = agg_node / jnp.maximum(cnt, 1.0)[:, None]
        feat = _gelu(jnp.concatenate([agg_node, H], axis=1))
        out = feat @ W2.T + b2
        return out

    def _L2_gnn_ref(h, w, src, dst, W1, b1, W2, b2, U1, c1, U2, c2):
        import jax, jax.numpy as jnp
        import numpy as np
        N = 12500
        E = 100000
        D = 128
        n = h.shape[0]
        msg_in = jnp.concatenate([h[src], h[dst], w[:, None]], axis=1)
        msg = jax.nn.relu(msg_in @ W1 + b1) @ W2 + b2
        agg = jax.ops.segment_max(msg, dst, num_segments=n)
        deg = jax.ops.segment_sum(jnp.ones((dst.shape[0],), jnp.int32), dst, num_segments=n)
        agg = jnp.where((deg > 0)[:, None], agg, jnp.zeros((), h.dtype))
        upd_in = jnp.concatenate([h, agg], axis=1)
        return jax.nn.relu(upd_in @ U1 + c1) @ U2 + c2

    def _L3_gnn_ref(x, edge_index, W_msg, b_msg, W_att, b_att, W_ih, b_ih, W_hh, b_hh, gamma, beta):
        import jax, jax.numpy as jnp
        import numpy as np
        N_NODES = 6250
        N_EDGES = 100000
        DIM = 128
        BN_EPS = 1e-05
        num_nodes, d = x.shape
        src = edge_index[0]
        dst = edge_index[1]
        xs = x[src]
        xd = x[dst]
        att = jax.nn.sigmoid(xs @ W_att[:d] + xd @ W_att[d:] + b_att)
        messages = (xs @ W_msg + b_msg) * att
        aggregated = jax.ops.segment_sum(messages, dst, num_segments=num_nodes)
        gi = aggregated @ W_ih.T + b_ih
        gh = x @ W_hh.T + b_hh
        i_r, i_z, i_n = jnp.split(gi, 3, axis=1)
        h_r, h_z, h_n = jnp.split(gh, 3, axis=1)
        r = jax.nn.sigmoid(i_r + h_r)
        z = jax.nn.sigmoid(i_z + h_z)
        n = jnp.tanh(i_n + r * h_n)
        h_new = (1.0 - z) * n + z * x
        mean = jnp.mean(h_new, axis=0)
        var = jnp.var(h_new, axis=0)
        return gamma * (h_new - mean) * jax.lax.rsqrt(var + BN_EPS) + beta
    edge_index = jnp.stack([src, dst])
    h = jnp.maximum(_layernorm(x, axis=-1), 0.0)
    x = x + _L0_gnn_ref(h, edge_index, L0_gnn_W_pre, L0_gnn_b_pre, L0_gnn_W_conv, L0_gnn_b_conv, L0_gnn_W_upd, L0_gnn_b_upd)
    h = jnp.maximum(_layernorm(x, axis=-1), 0.0)
    x = x + _L1_gnn_ref(h, edge_index, L1_gnn_W1, L1_gnn_b1, L1_gnn_WA, L1_gnn_WB, L1_gnn_W2, L1_gnn_b2)
    h = jnp.maximum(_layernorm(x, axis=-1), 0.0)
    x = x + _L2_gnn_ref(h, edge_weight, src, dst, L2_gnn_W1, L2_gnn_b1, L2_gnn_W2, L2_gnn_b2, L2_gnn_U1, L2_gnn_c1, L2_gnn_U2, L2_gnn_c2)
    h = jnp.maximum(_layernorm(x, axis=-1), 0.0)
    x = x + _L3_gnn_ref(h, edge_index, L3_gnn_W_msg, L3_gnn_b_msg, L3_gnn_W_att, L3_gnn_b_att, L3_gnn_W_ih, L3_gnn_b_ih, L3_gnn_W_hh, L3_gnn_b_hh, L3_gnn_gamma, L3_gnn_beta)
    return x

_drawn_inputs = setup_inputs


def setup_inputs(seed=0):
    import zlib

    import numpy as np

    out = dict(_drawn_inputs(seed))
    spreads = {'L0_gnn_b_pre': (0.0, 0.1),
     'L0_gnn_b_conv': (0.0, 0.1),
     'L0_gnn_b_upd': (0.0, 0.1),
     'L2_gnn_b1': (0.0, 0.1),
     'L2_gnn_b2': (0.0, 0.1),
     'L2_gnn_c1': (0.0, 0.1),
     'L2_gnn_c2': (0.0, 0.1),
     'L3_gnn_gamma': (1.0, 0.2),
     'L3_gnn_beta': (0.0, 0.1)}
    factors = {}
    for name, (base, spread) in spreads.items():
        noise = np.random.default_rng([zlib.crc32(name.encode()), seed]).standard_normal(out[name].shape)
        drawn = base * np.exp(spread * noise) if base else spread * noise
        out[name] = jnp.asarray(drawn.astype(out[name].dtype))
    for name, factor in factors.items():
        out[name] = (out[name] * factor).astype(out[name].dtype)
    return out
```

```python
import concourse.bass as bass
from concourse import mybir
from contextlib import ExitStack

D = 128
N = 6250
E = 100000
P = 128
BLOCKS = -(-N // P)
NP_ = BLOCKS * P
TILES = -(-E // P)
GROUP = 4
RING = 16
SLOTS = -(-(TILES + BLOCKS - 1) // RING) * RING
SJ = -(-(SLOTS + GROUP) // P)
SPAD = SJ * P
TPAD = SJ * P
QUADS = SLOTS // GROUP
QPL = RING // GROUP
CREDIT = RING + GROUP
LOOPS = SLOTS // RING
CB = 7
CH = CB * P
CHUNKS = BLOCKS // CB
MIX = 4
LAYERS = 3
ONES = 160
W_L1 = ONES + MIX
W_L3 = D + 4
EPS = 1e-5
FAR = -10000.0
LOW = -3.0e38

MATS_A0 = ["pre", "c0", "c1", "c2", "n0", "n1", "n2", "s0", "s1", "s2"]
MATS_A3 = ["msg", "ir", "iz", "in", "hr", "hz", "hn", "att_d"]
MATS_B = ["W1", "WA", "o_agg", "o_H", "W1s", "W1d", "W2", "U1h", "U1a", "U2"]
COLS = ["pre", "c0", "c1", "c2", "u0", "u1", "u2", "g_b1", "b2", "c1_", "att", "r", "z", "in", "hn", "r2", "z2", "gamma", "beta"]
ROWS = ["pre", "o1", "b1", "o2", "msg"]

STAGES = [("off", "V", 1), ("slot", "V", 1), ("t_idx", "V", 1), ("t_dl0", "A", 1), ("t_dl", "V", 1), ("t_dlL", "A", 1),
          ("ln0", "A", CHUNKS), ("pre_rows", "V", CHUNKS), ("pre_T", "A", CHUNKS)]
for _l in range(LAYERS):
    STAGES += [(f"xn{_l}", "A", CHUNKS), (f"h{_l}", "A", CHUNKS), (f"rows{_l}", "V", CHUNKS)]
STAGES += [("ln1", "A", CHUNKS), ("H", "A", CHUNKS), ("G", "A", CHUNKS), ("t1", "V", CHUNKS),
           ("mix", "V", CHUNKS * MIX), ("o1", "V", CHUNKS),
           ("ln2", "A", CHUNKS), ("t2", "A", CHUNKS), ("hb", "V", CHUNKS), ("u", "A", CHUNKS), ("o2", "V", CHUNKS),
           ("ln3", "A", CHUNKS), ("t3", "V", CHUNKS), ("ad", "A", CHUNKS),
           ("r", "A", CHUNKS), ("z", "A", CHUNKS), ("hn", "A", CHUNKS), ("in", "V", CHUNKS), ("o3", "V", CHUNKS)]
EVAC = [e for _, e, n in STAGES for _ in range(n)]
FIRST = {}
_u = 0
for _name, _, _n in STAGES:
    FIRST[_name] = _u
    _u += _n


def evacs(u):
    return EVAC[:u + 1].count(EVAC[u])


PASSES = ["L0a", "L0b", "L0c", "L1", "L2", "L3"]


def gnn(nc, io, out, debug=None):
    fp32, i32, bf16 = mybir.dt.float32, mybir.dt.int32, mybir.dt.bfloat16
    DVE = mybir.EngineType.DVE
    ALU, ACT = mybir.AluOpType, mybir.ActivationFunctionType

    ctx = ExitStack()
    with ctx:
        def sb(name, shape, dt=fp32):
            return ctx.enter_context(nc.sbuf_tensor(name, shape, dt))

        def sem(name):
            return ctx.enter_context(nc.semaphore(name))

        def dram(name, shape, dt=fp32):
            return nc.dram_tensor(name, shape, dt)

        tab0 = [dram(f"tab_L0_{l}", [NP_, D]) for l in range(LAYERS)]
        tab1 = dram("tab_L1", [NP_, W_L1])
        tab2 = dram("tab_L2", [NP_, D])
        tab3 = dram("tab_L3", [NP_, W_L3])
        x_keep = dram("x_keep", [NP_, D])
        blk_d = dram("blk_d", [SPAD], i32)
        rows_d = dram("rows_d", [2, SPAD, P])
        w_d = dram("w_d", [9, SPAD, P], bf16)
        c_d = dram("c_d", [3, D], bf16)

        pl = sb("planes", [P, 6, NP_])
        chunk = lambda p, c: pl[:, p, c * CH:(c + 1) * CH]
        block_of = lambda p, b: pl[:, p, b * P:(b + 1) * P]

        ring = sb("ring", [P, RING, W_L1])
        onehot = sb("onehot", [P, 2, GROUP, P])
        scaled = sb("scaled", [P, 4, MIX * P])
        idxT = sb("idxT", [P, SPAD], i32)
        idx_now = sb("idx_now", [P, 2, RING], i32)
        dlT = sb("dlT", [P, SPAD])
        dl0T = sb("dl0T", [P, SPAD])
        dlLT = sb("dlLT", [P, SPAD])
        blk = sb("blk", [1, SPAD], i32)
        cst = sb("cst", [P, 2 * P])
        slot_id = sb("slot_id", [P, SJ])
        matA = sb("matA", [P, len(MATS_A0), D])
        matB = sb("matB", [P, len(MATS_B), D])
        cols = sb("cols", [P, len(COLS)])
        brow = sb("brow", [P, len(ROWS), D])
        pick = sb("pick", [MIX, MIX, P])
        c9 = sb("c9", [9, D], bf16)
        bn = sb("bn", [P, 2 * CHUNKS, 6])
        fin = sb("fin", [P, 8])
        side = sb("side", [P, 2, 4])
        st = sb("st", [P, BLOCKS, 6])
        stat = sb("stat", [P, 5, BLOCKS])
        small = sb("small", [P, 10, SJ])
        fl = sb("fl", [P, SJ, 2], i32)
        fli = sb("fli", [P, SJ, 2], i32)
        flf = sb("flf", [P, SJ, 2])
        nt = sb("nt", [P, SJ, 2])
        tsi = sb("tsi", [P, SJ], i32)
        bsi = sb("bsi", [P, SJ], i32)

        ident, iota = cst[:, 0:P], cst[:, P:2 * P]
        A = lambda name: matA[:, MATS_A0.index(name), :]
        A3 = lambda name: matA[:, MATS_A3.index(name), :]
        B = lambda name: matB[:, MATS_B.index(name), :]
        col = lambda name: cols[:, COLS.index(name):COLS.index(name) + 1]
        over_blocks = lambda name, k: brow[:, ROWS.index(name), :].rearrange("p (o d) -> p o d", o=1).broadcast_to([P, k, D])

        ps = ctx.enter_context(nc.psum_tensor("ps", [P, 8, 512], fp32))
        flat = ps[:, :, :].rearrange("p b n -> p (b n)")
        unit = lambda u, n=CH: flat[:, (u % 4) * 1024:(u % 4) * 1024 + n]

        ld_first, ld_cst, ld_x, ld_wA, ld_wB, ld_misc = (sem(f"ld_{n}") for n in ("first", "cst", "x", "wA", "wB", "misc"))
        ld_slots = sem("ld_slots")
        st_slots = sem("st_slots")
        ld_blk = sem("ld_blk")
        tab_written = sem("tab_written")
        x_moved = sem("x_moved")
        maxed = sem("maxed")
        sw_ready = sem("sw_ready")
        bn_ready = sem("bn_ready")
        dve_setup = sem("dve_setup")
        node_done = sem("node_done")
        out_A, out_V = sem("out_A"), sem("out_V")
        normed = sem("normed")
        sqrt_in, sqrt_out = sem("sqrt_in"), sem("sqrt_out")
        gathered = [sem(f"gathered{q}") for q in range(QPL)]
        idx_ready = [sem(f"idx_ready{h}") for h in range(2)]
        sel_ready = sem("sel_ready")
        mm_done = sem("mm_done")
        acc_done = sem("acc_done")
        scaled_ready = sem("scaled_ready")
        sig_ready = sem("sig_ready")
        rows_in = [sem(f"rows_in{q}") for q in range(QPL)]
        st_ready = sem("st_ready")
        pre_done = sem("pre_done")
        hid_out = sem("hid_out")
        hidT_done = sem("hidT_done")
        hidT_out = sem("hidT_out")
        msg_done = sem("msg_done")
        msg_out = sem("msg_out")
        run_ready = sem("run_ready")
        runT_done = sem("runT_done")
        runT_out = sem("runT_out")
        pooled = sem("pooled")
        elem = sem("elem")
        gated = sem("gated")
        x_back = sem("x_back")
        c_moved = sem("c_moved")
        zeroed = sem("zeroed")
        passed = sem("passed")
        done = sem("done")

        block = ctx.enter_context(nc.Block())

        out_sem = {"A": out_A, "V": out_V}

        def free_banks(pe, u):
            if u >= 4:
                pe.wait_ge(out_sem[EVAC[u - 4]], evacs(u - 4))

        def await_out(eng, name, c):
            u = FIRST[name] + c
            eng.wait_ge(out_sem[EVAC[u]], evacs(u))

        def await_unit(eng, name, c):
            eng.wait_ge(node_done, FIRST[name] + c + 1)

        XP = {"L0": 5, "L1": 5, "L2": 1, "L3": 1}
        rows_view = lambda p, w=D: pl[:, p, :].rearrange("p (b d) -> p b d", d=w)
        dram_rows = lambda t: t[:, :].rearrange("(b p) d -> p b d", p=P)

        iota_s = pl[:, 4, 0:SPAD]
        cmp = pl[:, 0, :].rearrange("p (k s) -> p k s", s=SPAD)
        got = pl[:, 1, 0:SJ * 4 * P].bitcast(i32).rearrange("p (j c e) -> p j c e", j=SJ, c=4)
        got_w = pl[:, 2, 0:SJ * P].rearrange("p (j e) -> p j e", j=SJ)
        gotf = pl[:, 3, 0:SJ * 4 * P].rearrange("p (j c e) -> p j c e", j=SJ, c=4)
        base = 4 * SJ * P
        tmpw = lambda n, k=1: pl[:, n, base:base + k * SJ * P]
        eq = tmpw(1).rearrange("p (j e) -> p j e", j=SJ)
        rr = pl[:, 2, SJ * P:3 * SJ * P].rearrange("p (j c e) -> p j c e", j=SJ, c=2)
        dl0r = pl[:, 2, 3 * SJ * P:4 * SJ * P].rearrange("p (j e) -> p j e", j=SJ)
        dlLr = pl[:, 2, 4 * SJ * P:5 * SJ * P].rearrange("p (j e) -> p j e", j=SJ)
        dlr = pl[:, 2, 5 * SJ * P:6 * SJ * P].rearrange("p (j e) -> p j e", j=SJ)
        wpart = pl[:, 4, SPAD:SPAD + 2 * SJ * P].bitcast(bf16).rearrange("p (k j e) -> p k j e", k=4, j=SJ)
        rest = pl[:, 4, 3 * SPAD:4 * SPAD].rearrange("p (j e) -> p j e", j=SJ)
        upper, ones = (pl[:, 4, 4 * SPAD + k * P:4 * SPAD + (k + 1) * P] for k in range(2))
        cw = pl[0:1, 4, 5 * SPAD:5 * SPAD + 2 * D].rearrange("p (c d) -> p c d", c=2)
        cpart = pl[0:1, 4, 5 * SPAD + 2 * D:5 * SPAD + 4 * D].bitcast(bf16).rearrange("p (c d) -> p c d", c=4)[:, 0:3, :]
        counts = scaled[0:MIX, 0:2, :].rearrange("p a n -> p (a n)")[:, 0:CH]
        SM = lambda i: small[:, i, :]
        srcf, dstf, dprevf, dnextf = (gotf[:, :, c, :] for c in range(4))

        part = lambda plane, n, k: pl[:, plane, n * 512:(n + k) * 512]
        selT = part(3, 0, 2).rearrange("p (t n) -> p t n", t=2)
        hid = part(3, 2, 2).rearrange("p (t g n) -> p t g n", t=2, g=GROUP)
        hidT, msg = part(3, 4, 1), part(3, 5, 1)
        run = part(3, 6, 2).rearrange("p (t n) -> p t n", t=2)
        runT = part(3, 8, 1).rearrange("p (g n) -> p g n", g=GROUP)
        rowbc = part(4, 0, 2 * QPL).rearrange("p (q c n) -> p q c n", q=QPL, c=2)
        w9 = part(4, 2 * QPL, QPL // 2).bitcast(bf16).rearrange("p (q n) -> p q n", q=QPL)
        sig = scaled

        def used(p, s):
            return s + (CREDIT + p * SLOTS + 1)

        def added(p, s):
            return s + (CREDIT + p * (SLOTS + 1) + 2)

        def selected(p, q):
            return q + (p * (QUADS + 1) - (1 if p > 4 else 0) + 1)

        def blocks_at(engine, slot):
            return nc.values_load_multi_w_load_instructions(
                blk[0:1, bass.ds(slot, GROUP)], engines=[engine], min_val=0, max_val=NP_ - P,
                skip_runtime_bounds_check_because="the set-up clamps them")[1]

        def stages_of(it, q, lag):
            if isinstance(it, str):
                return q < lag
            return q >= lag if isinstance(it, int) else True

        @block.sync
        def _(sp):
            sp.dma_start(fl[:, :, :], io["ends"]).then_inc(ld_first, 16)
            sp.dma_start(cst[:, :], io["cst"][:, 0:2 * P]).then_inc(ld_cst, 16)
            sp.dma_start(pl[:, 4, 4 * SPAD:4 * SPAD + 2 * P], io["cst"][:, 2 * P:4 * P]).then_inc(ld_cst, 16)
            sp.dma_start(slot_id[:, :], io["cst"][:, 4 * P:4 * P + SJ]).then_inc(ld_cst, 16)
            sp.dma_start(iota_s, io["cst"][:, 4 * P + SJ:4 * P + SJ + SPAD]).then_inc(ld_cst, 16)
            sp.dma_start(rows_view(5), io["x"].rearrange("(b p) d -> p b d", p=P)).then_inc(ld_x, 16)
            sp.dma_start(matA[:, :, :], io["matsA0"]).then_inc(ld_wA, 16)
            sp.dma_start(cols[:, :], io["cols"]).then_inc(ld_misc, 16)
            sp.dma_start(side[:, :, :], io["side"]).then_inc(ld_misc, 16)
            sp.dma_start(brow[:, :, :], io["brow"].rearrange("(o r) d -> o r d", o=1).broadcast_to([P, len(ROWS), D])).then_inc(ld_misc, 16)
            sp.dma_start(pick[:, :, :], io["pick"]).then_inc(ld_misc, 16)
            sp.dma_start(cw[:, 0, :], io["w1c"]).then_inc(ld_misc, 16)
            sp.dma_start(matB[:, :, :], io["matsB"]).then_inc(ld_wB, 16)
            sp.wait_ge(dve_setup, 14)
            sp.dma_start(blk_d[:].rearrange("(j q) -> q j", q=P), bsi[:, :], allow_slow_non_contiguous=True).then_inc(st_slots, 16)
            sp.wait_ge(st_slots, 16)
            sp.dma_start(blk[0:1, :], blk_d[:].rearrange("(o s) -> o s", o=1)).then_inc(ld_blk, 16)
            sp.wait_ge(dve_setup, 23)
            for c in range(2):
                sp.dma_start(rows_d[c].rearrange("(j q) e -> q j e", q=P), rr[:, :, c, :]).then_inc(st_slots, 16)
            sp.wait_ge(dve_setup, 28)
            for k in range(9):
                sp.dma_start(w_d[k].rearrange("(j q) e -> q j e", q=P), wpart[:, k // 3]).then_inc(st_slots, 16)
            sp.wait_ge(dve_setup, 33)
            sp.dma_start(c_d[:, :].rearrange("(o c) d -> o c d", o=1), cpart[:, :, :]).then_inc(st_slots, 16)
            sp.wait_ge(st_slots, 16 * 13)
            for k in range(3):
                sp.dma_start(c9[3 * k:3 * k + 3, :], c_d[:, :]).then_inc(c_moved, 16)

            def table(stage, t, plane, w=D):
                both = pl[:, plane:plane + 2, :].rearrange("p a n -> p (a n)")
                for c in range(CHUNKS):
                    await_out(sp, stage, c)
                    sp.dma_start(dram_rows(t)[:, c * CB:(c + 1) * CB, :],
                                 both[:, c * CB * w:(c + 1) * CB * w].rearrange("p (b d) -> p b d", d=w)).then_inc(tab_written, 16)

            def stage_idx(p, it, h):
                sp.wait_ge(mm_done, used(p, it * RING - RING - 1))
                sp.dma_start(idx_now[:, h, :], idxT[:, bass.ds(it * RING, RING)]).then_inc(idx_ready[h], 16)

            def stage_all(p):
                with sp.Fori(0, LOOPS // 2) as i:
                    for h in range(2):
                        stage_idx(p, i * 2 + h, h)

            def load_rows(it, q):
                sp.wait_ge(run_ready, it * QPL + q + 1)
                s0 = it * RING + q * GROUP
                sp.dma_start(rowbc[:, q], rows_d[:, bass.ds(s0, GROUP), :].rearrange("(o c) g e -> o c (g e)", o=1).broadcast_to([P, 2, GROUP * P])
                             ).then_inc(rows_in[q], 16)
                sp.dma_start(w9[0:9, q, :], w_d[:, bass.ds(s0, GROUP), :].rearrange("k g e -> k (g e)")).then_inc(rows_in[q], 16)

            await_out(sp, "t_idx", 0)
            table("pre_rows", tab0[0], 3)
            stage_all(0)
            table("rows0", tab0[1], 3)
            stage_all(1)
            table("rows1", tab0[2], 3)
            stage_all(2)
            for c in range(CHUNKS):
                sp.wait_ge(elem, c + 1)
                sp.dma_start(dram_rows(x_keep)[:, c * CB:(c + 1) * CB, :], rows_view(2)[:, c * CB:(c + 1) * CB, :]).then_inc(x_moved, 16)
            table("t1", tab1, 3, W_L1)
            stage_all(3)
            sp.wait_ge(x_moved, 16 * CHUNKS)
            for c in range(CHUNKS):
                sp.wait_ge(pooled, 3 * c + 1)
                sp.dma_start(rows_view(1)[:, c * CB:(c + 1) * CB, :], dram_rows(x_keep)[:, c * CB:(c + 1) * CB, :]).then_inc(x_back, 16)
            sp.dma_start(matA[:, 0:len(MATS_A3), :], io["matsA3"]).then_inc(ld_wA, 16)
            table("t2", tab2, 4)
            sp.wait_ge(tab_written, 16 * CHUNKS * 5)
            stage_idx(4, 0, 0)
            with sp.Fori(0, LOOPS // 2) as i:
                for h in range(2):
                    it = i * 2 + h
                    for q in range(QPL - 1):
                        load_rows(it, q)
                    stage_idx(4, it + 1, 1 - h)
                    load_rows(it, QPL - 1)
            load_rows(LOOPS, 0)
            sp.wait_ge(idx_ready[0], 16 * (5 * LOOPS // 2 + 1))
            table("t3", tab3, 3, W_L3)
            stage_all(5)
            for c in range(CHUNKS):
                await_out(sp, "o3", c)
                sp.dma_start(out.rearrange("(b p) d -> p b d", p=P)[:, c * CB:(c + 1) * CB, :], rows_view(1)[:, c * CB:(c + 1) * CB, :]).then_inc(done, 16)
            sp.wait_ge(done, 16 * CHUNKS)

        @block.gpsimd
        def _(pool):
            pool.wait_ge(dve_setup, 9)
            for j in range(SJ):
                pool.indirect_dma_start(got[:, j, :, :].rearrange("p c e -> p (c e)"), None, io["edges"].rearrange("t c e -> t (c e)"),
                                        bass.IndirectOffsetOnAxis(tsi[:, j:j + 1], 0)).then_inc(ld_slots, 16)
            for j in range(SJ):
                pool.indirect_dma_start(got_w[:, j, :], None, io["weights"],
                                        bass.IndirectOffsetOnAxis(tsi[:, j:j + 1], 0)).then_inc(ld_slots, 16)

            def gather(p, table, width):
                pool.wait_ge(tab_written, 16 * CHUNKS * (p + 1))
                with pool.Fori(0, LOOPS // 2) as i:
                    for h in range(2):
                        pool.wait_ge(idx_ready[h], i * 16 + 16 * (p * (LOOPS // 2) + 1 + (1 if p > 4 and h == 0 else 0)))
                        pool.sem_inc(passed)
                        for q in range(QPL):
                            pool.wait_ge(mm_done, used(p, i * (2 * RING) + (h * RING + q * GROUP + GROUP - 1 - RING)))
                            pool.sem_inc(passed)
                            for g in range(GROUP):
                                s = q * GROUP + g
                                pool.indirect_dma_start(ring[:, s, 0:width], None, table[:, :],
                                                        bass.IndirectOffsetOnAxis(idx_now[:, h, s:s + 1], 0)).then_inc(gathered[q], 16)

            for l in range(LAYERS):
                gather(l, tab0[l], D)
            gather(3, tab1, W_L1)
            for c in range(CHUNKS):
                for n, (a, b, m) in enumerate(((0, 1, 1), (2, 3, 3), (0, 2, None))):
                    if m is None:
                        pool.wait_ge(pooled, 3 * c + 2)
                    else:
                        await_out(pool, "mix", MIX * c + m)
                    pool.tensor_tensor(chunk(a, c), chunk(a, c), chunk(b, c), ALU.add).then_inc(pooled, 1)
            gather(4, tab2, D)
            gather(5, tab3, W_L3)
            for c in range(CHUNKS):
                pool.wait_ge(gated, 6 * CHUNKS + c + 1)
                pool.tensor_tensor(chunk(3, c), chunk(2, c), chunk(5, c), ALU.subtract).then_inc(pooled, 1)

        @block.vector
        def _(dve):
            chain = [0]

            def link(ins):
                chain[0] += 1
                ins.then_inc(dve_setup, 1)
                dve.wait_ge(dve_setup, chain[0])

            dve.wait_ge(ld_first, 16)
            link(dve.tensor_scalar(fli[:, :, :], fl[:, :, :], 7, None, ALU.arith_shift_right))
            link(dve.tensor_copy(flf[:, :, :], fli[:, :, :]))
            link(dve.memset(nt[:, :, :], 1.0))
            link(dve.scalar_tensor_tensor(nt[:, :, 1], flf[:, :, 1], 1.0, flf[:, :, 0], ALU.add, ALU.subtract))
            link(dve.tensor_tensor_scan(SM(0), nt[:, :, 0], nt[:, :, 1], 0.0, ALU.mult, ALU.add))
            link(dve.tensor_tensor(SM(1), SM(0), nt[:, :, 1], ALU.subtract))
            await_unit(dve, "off", 0)
            dve.tensor_copy(SM(2), unit(FIRST["off"], SJ)).then_inc(out_V, 1)
            dve.wait_ge(out_V, 1)
            dve.wait_ge(ld_cst, 64)
            for k in range(SJ):
                last = dve.tensor_scalar(cmp[:, k, :], iota_s, small[:, 2, k:k + 1], None, ALU.is_ge)
            link(last)
            await_unit(dve, "slot", 0)
            dve.tensor_copy(small[:, 3:5, :].rearrange("p c j -> p j c"), unit(FIRST["slot"], 2 * SJ).rearrange("p (j c) -> p j c", c=2)).then_inc(out_V, 1)
            dve.wait_ge(out_V, 2)
            link(dve.tensor_scalar(SM(5), SM(3), 1.0, None, ALU.subtract))
            link(dve.tensor_copy(tsi[:, :], SM(5)))
            dve.wait_ge(ld_slots, 32 * SJ)
            link(dve.tensor_copy(gotf, got))
            link(dve.tensor_scalar(bsi[:, :], got[:, :, 1, P - 1], 7, None, ALU.arith_shift_right))
            link(dve.tensor_tensor(SM(6), SM(4), bsi[:, :], ALU.subtract))
            link(dve.scalar_tensor_tensor(SM(7), slot_id[:, :], 1.0, SM(6), ALU.add, ALU.subtract))
            link(dve.tensor_scalar(bsi[:, :], SM(7), float(BLOCKS - 1), float(P), ALU.min, ALU.mult))
            link(dve.tensor_scalar(SM(8), SM(7), float(P), None, ALU.mult))
            first = small[:, 8:9, :].rearrange("p o j -> p j o").broadcast_to([P, SJ, P])
            link(dve.tensor_tensor(dlr, dstf, first, ALU.subtract))
            link(dve.tensor_tensor(eq, srcf, dstf, ALU.is_equal))
            link(dve.scalar_tensor_tensor(dl0r, eq, FAR, dlr, ALU.mult, ALU.add))
            link(dve.tensor_tensor(eq, dstf, dnextf, ALU.is_equal))
            link(dve.scalar_tensor_tensor(dlLr, eq, FAR, dlr, ALU.mult, ALU.add))
            link(dve.tensor_tensor(eq, dstf, dprevf, ALU.not_equal))
            link(dve.tensor_scalar(rr[:, :, 1, :], eq, LOW, None, ALU.mult))
            link(dve.tensor_copy(rr[:, :, 0, :], dlr))
            link(dve.tensor_copy(wpart[:, 0], got_w))
            link(dve.tensor_tensor(rest, got_w, wpart[:, 0], ALU.subtract))
            link(dve.tensor_copy(wpart[:, 1], rest))
            link(dve.tensor_tensor(rest, rest, wpart[:, 1], ALU.subtract))
            link(dve.tensor_copy(wpart[:, 2], rest))
            dve.wait_ge(ld_misc, 80)
            link(dve.tensor_copy(cpart[:, 0, :], cw[:, 0, :]))
            link(dve.tensor_tensor(cw[:, 1, :], cw[:, 0, :], cpart[:, 0, :], ALU.subtract))
            link(dve.tensor_copy(cpart[:, 1, :], cw[:, 1, :]))
            link(dve.tensor_tensor(cw[:, 1, :], cw[:, 1, :], cpart[:, 1, :], ALU.subtract))
            link(dve.tensor_copy(cpart[:, 2, :], cw[:, 1, :]))
            await_unit(dve, "t_idx", 0)
            dve.tensor_copy(idxT[:, :], unit(FIRST["t_idx"], SPAD)).then_inc(out_V, 1)
            await_unit(dve, "t_dl", 0)
            dve.tensor_copy(dlT[:, :], unit(FIRST["t_dl"], SPAD)).then_inc(out_V, 1)

            for s_, n_ in ((mm_done, CREDIT), (acc_done, CREDIT), (run_ready, QPL), (hid_out, QPL), (hidT_done, QPL), (hidT_out, QPL),
                           (msg_done, QPL), (msg_out, QPL), (runT_done, QPL), (runT_out, QPL), (maxed, QPL)):
                dve.sem_inc(s_, n_)

            def layer_norm(n, xp, yp):
                X, Y = rows_view(xp), rows_view(yp)
                for b in range(BLOCKS):
                    last = dve.bn_stats(st[:, b, :], X[:, b, :])
                link(last)
                link(dve.tensor_tensor(stat[:, 0], st[:, :, 1], st[:, :, 4], ALU.add))
                link(dve.tensor_tensor(stat[:, 1], st[:, :, 1], st[:, :, 4], ALU.subtract))
                link(dve.tensor_tensor(stat[:, 2], st[:, :, 2], st[:, :, 5], ALU.add))
                link(dve.tensor_tensor(stat[:, 1], stat[:, 1], stat[:, 1], ALU.mult))
                link(dve.tensor_scalar(stat[:, 2], stat[:, 2], 1.0 / D, EPS, ALU.mult, ALU.add))
                link(dve.scalar_tensor_tensor(stat[:, 2], stat[:, 1], 0.25, stat[:, 2], ALU.mult, ALU.add))
                dve.tensor_scalar(stat[:, 0], stat[:, 0], 0.5, None, ALU.mult).then_inc(sqrt_in, 1)
                dve.wait_ge(sqrt_out, n + 1)
                link(dve.reciprocal(stat[:, 4], stat[:, 3]))
                for b in range(BLOCKS):
                    last = dve.tensor_scalar(Y[:, b, :], X[:, b, :], stat[:, 0, b:b + 1], stat[:, 4, b:b + 1], ALU.subtract, ALU.mult)
                    if b % CB == CB - 1:
                        last.then_inc(normed, 1)

            def rows_to(stage, plane, bias=None):
                for c in range(CHUNKS):
                    await_unit(dve, stage, c)
                    src = unit(FIRST[stage] + c).rearrange("p (b d) -> p b d", d=D)
                    dst = rows_view(plane)[:, c * CB:(c + 1) * CB, :]
                    if bias is None:
                        dve.tensor_copy(dst, src).then_inc(out_V, 1)
                    else:
                        dve.tensor_tensor(dst, src, over_blocks(bias, CB), ALU.add).then_inc(out_V, 1)

            def wide_rows(stage, plane, w, bias):
                both = pl[:, plane:plane + 2, :].rearrange("p a n -> p (a n)")[:, 0:BLOCKS * w].rearrange("p (b d) -> p b d", d=w)
                if w == W_L1:
                    dve.memset(both[:, :, D + MIX:ONES], 0.0)
                    dve.memset(both[:, :, ONES:w], 1.0)
                for c in range(CHUNKS):
                    await_unit(dve, stage, c)
                    src = unit(FIRST[stage] + c, CH).rearrange("p (b d) -> p b d", d=D)
                    dst = both[:, c * CB:(c + 1) * CB, 0:D]
                    if bias is None:
                        dve.tensor_copy(dst, src)
                    else:
                        dve.tensor_tensor(dst, src, over_blocks(bias, CB), ALU.add)
                    dve.tensor_copy(both[:, c * CB:(c + 1) * CB, D:D + 4],
                                    unit(FIRST[stage] + c, CH + 4 * CB)[:, CH:].rearrange("p (b d) -> p b d", d=4)).then_inc(out_V, 1)

            def add_to_x(stage, plane):
                for c in range(CHUNKS):
                    await_unit(dve, stage, c)
                    x = rows_view(plane)[:, c * CB:(c + 1) * CB, :]
                    dve.tensor_tensor(x, x, unit(FIRST[stage] + c).rearrange("p (b d) -> p b d", d=D), ALU.add).then_inc(out_V, 1)

            def bias_x(src, dst, bias, sem_=None):
                for c in range(CHUNKS):
                    ins = dve.tensor_tensor(rows_view(dst)[:, c * CB:(c + 1) * CB, :], rows_view(src)[:, c * CB:(c + 1) * CB, :],
                                            over_blocks(bias, CB), ALU.add)
                    if sem_ is not None:
                        ins.then_inc(sem_, 1)
                    else:
                        last = ins
                if sem_ is None:
                    link(last)

            def one_hots(dl, t, first_slot):
                a = iota.rearrange("p (o n) -> p o n", o=1).broadcast_to([P, GROUP, P])
                b = dl[:, bass.ds(first_slot, GROUP)].rearrange("p (g o) -> p g o", o=1).broadcast_to([P, GROUP, P])
                return dve.tensor_tensor(onehot[:, t % 2], a, b, ALU.is_equal)

            def add_group(p, it, s, bank, ready):
                first = blocks_at(DVE, it * RING + s)
                ready()
                for g in range(GROUP):
                    dve.wait_ge(acc_done, added(p, it * RING + (s + g - 1)))
                    at = pl[:, 0, bass.ds(first[g], P)]
                    dve.tensor_tensor(at, at, ps[:, bank, g * P:(g + 1) * P], ALU.add).then_inc(acc_done, 1)

            def sum_pass(p, dl):
                if p:
                    dve.wait_ge(sel_ready, selected(p, -1))
                one_hots(dl, 0, 0).then_inc(sel_ready, 1)
                dve.memset(pl[:, 0, :], 0.0).then_inc(acc_done, 1)
                with dve.Fori(0, LOOPS) as i:
                    for q in range(QPL):
                        one_hots(dl, q + 1, i * RING + (q + 1) * GROUP).then_inc(sel_ready, 1)
                        add_group(p, i, q * GROUP, q % 2, lambda: dve.wait_ge(mm_done, used(p, i * RING + (q * GROUP + GROUP - 1))))

            dve.wait_ge(ld_x, 16)
            layer_norm(0, 5, 3)
            rows_to("pre_rows", 3, "pre")
            dve.wait_ge(ld_blk, 16)
            for l in range(LAYERS):
                sum_pass(l, dl0T)
                if l < LAYERS - 1:
                    rows_to(f"rows{l}", 3)
            add_to_x("rows2", 5)
            dve.wait_ge(out_V, evacs(FIRST["rows2"] + CHUNKS - 1))

            layer_norm(1, 5, 3)
            bias_x(5, 2, "o1", elem)
            dve.memset(pl[:, 0, :], 0.0).then_inc(elem, 1)
            await_unit(dve, "t1", 0)
            wide_rows("t1", 3, W_L1, None)
            dve.wait_ge(x_moved, 16 * CHUNKS)
            dve.memset(pl[:, 2, :], 0.0)
            await_out(dve, "t1", CHUNKS - 1)
            for u in range(4):
                dve.memset(ps[:, 2 * u + 1, 0:P], 0.0)
            dve.wait_ge(sel_ready, selected(3, -1))
            one_hots(dlT, 0, 0).then_inc(sel_ready, 1)
            dve.wait_ge(tab_written, 16 * CHUNKS * 4)
            dve.memset(pl[:, 4, :], 0.0).then_inc(acc_done, 1)
            dve.wait_ge(zeroed, 2)
            with dve.Fori(0, LOOPS) as i:
                for q in range(QPL):
                    one_hots(dlT, q + 1, i * RING + (q + 1) * GROUP).then_inc(sel_ready, 1)
                    first = blocks_at(DVE, i * RING + q * GROUP)
                    for g in range(GROUP):
                        s = q * GROUP + g
                        dve.wait_ge(mm_done, used(3, i * RING + s))
                        dve.wait_ge(acc_done, added(3, i * RING + s - 1))
                        at = pl[:, 0:MIX + 1, bass.ds(first[g], P)]
                        dve.tensor_tensor(at, at, flat[:, (s % 4) * 1024:(s % 4) * 1024 + (MIX + 1) * P].rearrange("p (m n) -> p m n", n=P),
                                          ALU.add).then_inc(acc_done, 1)
            dve.wait_ge(acc_done, added(3, SLOTS - 1))
            for c in range(CHUNKS):
                cnt = pl[0:MIX, 4, 0:1]
                link(dve.tensor_scalar(counts, pl[32:32 + MIX, 4, c * CH:(c + 1) * CH], 1.0, None, ALU.max))
                link(dve.reciprocal(counts, counts))
                w = pl[0:MIX, 4, c * CH:(c + 1) * CH]
                dve.tensor_tensor(w, w, counts, ALU.mult).then_inc(sw_ready, 1)
                for m in range(MIX):
                    await_unit(dve, "mix", MIX * c + m)
                    dve.wait_ge(gated, 2 + MIX * c + m + 1 - 2)
                    dve.tensor_tensor(chunk(m, c), chunk(m, c), unit(FIRST["mix"] + MIX * c + m), ALU.mult).then_inc(out_V, 1)
            dve.wait_ge(x_back, 16 * CHUNKS)
            add_to_x("o1", 1)
            dve.wait_ge(out_V, evacs(FIRST["o1"] + CHUNKS - 1))

            layer_norm(2, 1, 3)
            dve.memset(pl[:, 0, :], 0.0).then_inc(acc_done, 1)
            dve.wait_ge(normed, 3 * CHUNKS)
            bias_x(1, 1, "o2")
            rows_to("hb", 5, "b1")

            def transposed_one_hots(it, q):
                dve.wait_ge(mm_done, used(4, it * RING + q * GROUP - 2 * GROUP + GROUP - 1))
                dve.wait_ge(rows_in[q % QPL], (it + (q // QPL)) * 32 + 32)
                dve.tensor_scalar(selT[:, q % 2, :], rowbc[:, q % QPL, 0, :], slot_id[:, 0:1], None, ALU.is_equal).then_inc(st_ready, 1)

            transposed_one_hots(0, 0)

            def max_step(it, q):
                at = LOOPS if isinstance(it, str) else it
                T = at * QPL + q
                if stages_of(it, q, 2):
                    one_hots(dlLT, q, at * RING + (q - 2) * GROUP).then_inc(sel_ready, 1)
                if stages_of(it, q, 3):
                    add_group(4, at, (q - 3) * GROUP, 5 + (q - 3) % 2, lambda: dve.wait_ge(maxed, T + (QPL - 2)))
                if not isinstance(it, str):
                    transposed_one_hots(at, q + 1)
                if stages_of(it, q, 1):
                    dve.wait_ge(msg_out, T + QPL)
                    dve.wait_ge(runT_done, T + (QPL - 2))
                    dve.wait_ge(run_ready, T + (QPL - 1))
                    before = LOW if (isinstance(it, int) and q == 1) else run[:, q % 2, GROUP * P - 1:GROUP * P]
                    dve.tensor_tensor_scan(run[:, (q - 1) % 2, :], rowbc[:, (q - 1) % QPL, 1, :], msg, before, ALU.add, ALU.max).then_inc(run_ready, 1)

            for q in range(QPL):
                max_step(0, q)
            with dve.Fori(1, LOOPS) as i:
                for q in range(QPL):
                    max_step(i, q)
            for q in range(3):
                max_step("end", q)
            add_to_x("o2", 1)
            dve.wait_ge(out_V, evacs(FIRST["o2"] + CHUNKS - 1))

            layer_norm(3, 1, 3)
            dve.wait_ge(acc_done, added(5, -2))
            dve.memset(pl[:, 0, :], 0.0).then_inc(acc_done, 1)
            dve.tensor_tensor(col("r"), col("r"), col("r2"), ALU.add).then_inc(elem, 1)
            dve.tensor_tensor(col("z"), col("z"), col("z2"), ALU.add).then_inc(elem, 1)
            wide_rows("t3", 3, W_L3, "msg")

            def weighted(it, q):
                dve.wait_ge(sig_ready, it * QPL + q + 1)
                for g in range(GROUP):
                    last = dve.scalar_tensor_tensor(onehot[:, q % 2, g, :], iota, dlT[:, bass.ds(it * RING + q * GROUP + g, 1)],
                                                    sig[:, q % 4, g * P:(g + 1) * P], ALU.is_equal, ALU.mult)
                last.then_inc(sel_ready, 1)

            dve.wait_ge(sel_ready, selected(5, -1))
            weighted(0, 0)
            with dve.Fori(0, LOOPS) as i:
                for q in range(QPL):
                    weighted(i, q + 1)
                    add_group(5, i, q * GROUP, q % 2, lambda: dve.wait_ge(mm_done, used(5, i * RING + (q * GROUP + GROUP - 1))))
            for c in range(CHUNKS):
                await_out(dve, "hn", c)
                link(dve.tensor_tensor(chunk(3, c), chunk(3, c), chunk(5, c), ALU.mult))
                await_unit(dve, "in", c)
                dve.tensor_tensor(chunk(5, c), chunk(3, c), unit(FIRST["in"] + c), ALU.add).then_inc(out_V, 1)
            for c in range(CHUNKS):
                dve.wait_ge(pooled, 3 * CHUNKS + c + 1)
                link(dve.tensor_tensor(chunk(3, c), chunk(3, c), chunk(4, c), ALU.mult))
                link(dve.tensor_tensor(chunk(3, c), chunk(3, c), chunk(5, c), ALU.add))
                n = min(CH, N - c * CH) // 2
                for k in range(2):
                    last = dve.bn_stats(bn[:, 2 * c + k, :], chunk(3, c)[:, k * n:(k + 1) * n])
            link(last)
            link(dve.bn_aggr(fin[:, 0:2], bn[:, :, :].rearrange("p a b -> p (a b)")))
            dve.tensor_scalar(fin[:, 2:3], fin[:, 1:2], EPS, None, ALU.add).then_inc(sqrt_in, 1)
            dve.wait_ge(sqrt_out, 5)
            link(dve.reciprocal(fin[:, 4:5], fin[:, 3:4]))
            link(dve.tensor_tensor(fin[:, 5:6], fin[:, 4:5], col("gamma"), ALU.mult))
            link(dve.tensor_tensor(fin[:, 6:7], fin[:, 0:1], fin[:, 5:6], ALU.mult))
            dve.tensor_tensor(fin[:, 7:8], col("beta"), fin[:, 6:7], ALU.subtract).then_inc(bn_ready, 1)
            add_to_x("o3", 1)

        @block.scalar
        def _(act):
            act.wait_ge(ld_misc, 80)

            def from_psum(stage, dst, func, bias=None, ready=lambda c: None):
                for c in range(CHUNKS):
                    ready(c)
                    await_unit(act, stage, c)
                    if bias is None:
                        act.activation(dst(c), unit(FIRST[stage] + c), func).then_inc(out_A, 1)
                    else:
                        act.activation(dst(c), unit(FIRST[stage] + c), func, bias=col(bias)).then_inc(out_A, 1)

            await_unit(act, "t_dl0", 0)
            act.activation(dl0T[:, :], unit(FIRST["t_dl0"], SPAD), ACT.Copy).then_inc(out_A, 1)
            await_unit(act, "t_dlL", 0)
            act.activation(dlLT[:, :], unit(FIRST["t_dlL"], SPAD), ACT.Copy).then_inc(out_A, 1)

            def root(n):
                act.wait_ge(sqrt_in, n + 1)
                act.activation(stat[:, 3], stat[:, 2], ACT.Sqrt).then_inc(sqrt_out, 1)

            root(0)
            act.wait_ge(st_slots, 16 * 13)
            from_psum("ln0", lambda c: chunk(4, c), ACT.Relu)
            from_psum("pre_T", lambda c: chunk(2, c), ACT.Identity, "pre")
            for l in range(LAYERS):
                from_psum(f"xn{l}", lambda c: chunk(1, c), ACT.Identity, f"c{l}")
                from_psum(f"h{l}", lambda c: chunk(2, c), ACT.Relu, f"u{l}")

            root(1)
            from_psum("ln1", lambda c: chunk(4, c), ACT.Relu)
            act.wait_ge(elem, CHUNKS)
            from_psum("H", lambda c: chunk(5, c), ACT.Gelu, "g_b1")
            from_psum("G", lambda c: chunk(1, c), ACT.Gelu)
            act.wait_ge(elem, CHUNKS + 1)
            await_unit(act, "t1", CHUNKS - 1)
            act.activation(pl[:, 1, :], pl[:, 0, :], ACT.Copy).then_inc(zeroed, 1)
            act.wait_ge(tab_written, 16 * CHUNKS * 4)
            act.activation(pl[:, 3, :], pl[:, 0, :], ACT.Copy).then_inc(zeroed, 1)
            with act.Fori(0, LOOPS) as i:
                for q in range(QPL):
                    act.wait_ge(gathered[q], i * (16 * GROUP) + 16 * GROUP * (3 * LOOPS + 1))
                    act.wait_ge(sel_ready, selected(3, i * QPL + q))
                    for g in range(GROUP):
                        s = q * GROUP + g
                        act.wait_ge(mm_done, used(3, i * RING + s - 4))
                        for m in range(MIX):
                            last = act.activation(scaled[:, s % 4, m * P:(m + 1) * P], onehot[:, q % 2, g, :], ACT.Copy,
                                                  scale=ring[:, s, D + m:D + m + 1])
                        last.then_inc(scaled_ready, 1)
            act.wait_ge(acc_done, added(3, SLOTS - 1))
            for c in range(CHUNKS):
                for m in range(MIX):
                    act.activation(chunk(m, c), chunk(m, c), ACT.Gelu).then_inc(gated, 1)
            for c in range(CHUNKS):
                act.activation(chunk(5, c), chunk(5, c), ACT.Gelu).then_inc(gated, 1)
            for c in range(CHUNKS):
                act.wait_ge(pooled, 3 * (c + 1))
                act.activation(chunk(0, c), chunk(0, c), ACT.Gelu).then_inc(gated, 1)

            root(2)
            from_psum("ln2", lambda c: chunk(2, c), ACT.Relu)
            from_psum("t2", lambda c: chunk(4, c), ACT.Copy)

            def max_step(it, q):
                at = LOOPS if isinstance(it, str) else it
                T = at * QPL + q
                if not isinstance(it, str):
                    act.wait_ge(mm_done, used(4, at * RING + q * GROUP + GROUP - 1))
                    act.wait_ge(hidT_done, T + (QPL - 1))
                    act.activation(hid[:, q % 2], ps[:, q % 2, :].rearrange("p (g n) -> p g n", g=GROUP), ACT.Relu).then_inc(hid_out, 1)
                if stages_of(it, q, 1):
                    act.wait_ge(hidT_done, T + QPL)
                    act.wait_ge(msg_done, T + (QPL - 1))
                    act.activation(hidT, ps[:, 2, :], ACT.Copy).then_inc(hidT_out, 1)
                    act.wait_ge(msg_done, T + QPL)
                    act.wait_ge(run_ready, T + (QPL - 1))
                    act.activation(msg, ps[:, 3, :], ACT.Identity, bias=col("b2")).then_inc(msg_out, 1)
                if stages_of(it, q, 2):
                    act.wait_ge(runT_done, T + (QPL - 1))
                    act.wait_ge(maxed, T + (QPL - 2))
                    act.activation(runT[:, :, :], ps[:, 4, :].rearrange("p (g n) -> p g n", g=GROUP), ACT.Copy).then_inc(runT_out, 1)

            for q in range(QPL):
                max_step(0, q)
            with act.Fori(1, LOOPS) as i:
                for q in range(QPL):
                    max_step(i, q)
            for q in range(3):
                max_step("end", q)
            from_psum("u", lambda c: chunk(3, c), ACT.Relu, "c1_")

            root(3)
            from_psum("ln3", lambda c: chunk(2, c), ACT.Relu)
            from_psum("ad", lambda c: chunk(5, c), ACT.Identity, "att")
            act.wait_ge(ld_blk, 16)

            def attention(it, q):
                act.wait_ge(gathered[q % QPL], (it + q // QPL) * (16 * GROUP) + 16 * GROUP * (5 * LOOPS + 1))
                act.wait_ge(sel_ready, selected(5, it * QPL + q - 4))
                first = blocks_at(mybir.EngineType.Activation, it * RING + q * GROUP)
                for g in range(GROUP):
                    s = q * GROUP + g
                    last = act.activation(sig[:, q % 4, g * P:(g + 1) * P], pl[:, 5, bass.ds(first[g], P)], ACT.Sigmoid,
                                          bias=ring[:, s % RING, D:D + 1])
                last.then_inc(sig_ready, 1)

            with act.Fori(0, LOOPS) as i:
                for q in range(QPL):
                    attention(i, q)
            act.wait_ge(sel_ready, selected(5, QUADS - 4))
            act.activation(sig[:, 0, :], pl[:, 5, 0:512], ACT.Copy).then_inc(sig_ready, 1)
            act.wait_ge(elem, CHUNKS + 3)
            from_psum("r", lambda c: chunk(3, c), ACT.Sigmoid, "r")
            from_psum("z", lambda c: chunk(4, c), ACT.Sigmoid, "z")
            from_psum("hn", lambda c: chunk(5, c), ACT.Identity, "hn")
            for c in range(CHUNKS):
                await_out(act, "in", c)
                act.activation(chunk(5, c), chunk(5, c), ACT.Tanh, bias=col("in")).then_inc(gated, 1)
            act.wait_ge(sqrt_in, 5)
            act.activation(fin[:, 3:4], fin[:, 2:3], ACT.Sqrt).then_inc(sqrt_out, 1)
            act.wait_ge(bn_ready, 1)
            for c in range(CHUNKS):
                act.activation(chunk(4, c), chunk(3, c), ACT.Identity, scale=fin[:, 5:6], bias=fin[:, 7:8]).then_inc(gated, 1)

        @block.tensor
        def _(pe):
            pe.wait_ge(ld_cst, 64)
            pe.wait_ge(dve_setup, 6)
            u = FIRST["off"]
            pe.matmul(unit(u, SJ), upper, nt[:, :, 1], start=True, stop=False)
            pe.matmul(unit(u, SJ), ones, SM(1), start=False, stop=True).then_inc(node_done, 1)
            pe.wait_ge(dve_setup, 7)
            u = FIRST["slot"]
            for j in range(SJ):
                for k in range(SJ):
                    last = pe.matmul(unit(u, 2 * SJ)[:, 2 * j:2 * j + 2], cmp[:, k, j * P:(j + 1) * P], nt[:, k, :],
                                     start=(k == 0), stop=(k == SJ - 1))
            last.then_inc(node_done, 1)
            for name, src, after in (("t_idx", srcf, 10), ("t_dl0", dl0r, 18), ("t_dl", dlr, 20), ("t_dlL", dlLr, 20)):
                pe.wait_ge(dve_setup, after)
                u = FIRST[name]
                free_banks(pe, u)
                for j in range(SJ):
                    last = pe.transpose(unit(u, SPAD)[:, j * P:(j + 1) * P], src[:, j, :], ident)
                last.then_inc(node_done, 1)

            def transposed(stage, plane, ready):
                for c in range(CHUNKS):
                    u = FIRST[stage] + c
                    free_banks(pe, u)
                    ready(c)
                    for b in range(CB):
                        last = pe.transpose(unit(u)[:, b * P:(b + 1) * P], block_of(plane, c * CB + b), ident)
                    last.then_inc(node_done, 1)

            def rows_of(stage, terms, ready, extra=None):
                for c in range(CHUNKS):
                    u = FIRST[stage] + c
                    free_banks(pe, u)
                    ready(c)
                    for b in range(CB):
                        for n, (plane, mat) in enumerate(terms):
                            last = pe.matmul(unit(u)[:, b * P:(b + 1) * P], block_of(plane, c * CB + b), mat,
                                             start=(n == 0), stop=(n == len(terms) - 1))
                    if extra:
                        last = four_more(u, c, *extra)
                    last.then_inc(node_done, 1)

            def four_more(u, c, plane, mat):
                for b in range(CB):
                    last = pe.matmul(unit(u, 1024)[:, CH + 4 * b:CH + 4 * b + 4], block_of(plane, c * CB + b), mat, start=True, stop=True)
                return last

            def product(stage, terms, ready):
                for c in range(CHUNKS):
                    u = FIRST[stage] + c
                    free_banks(pe, u)
                    ready(c)
                    for a, z in ((0, 512), (512, CH)):
                        for n, (mat, plane) in enumerate(terms):
                            last = pe.matmul(unit(u)[:, a:z], mat, chunk(plane, c)[:, a:z], start=(n == 0), stop=(n == len(terms) - 1))
                    last.then_inc(node_done, 1)

            def settled(*stages):
                for stage in stages:
                    await_out(pe, stage, CHUNKS - 1)

            def sum_edges(p):
                with pe.Fori(0, LOOPS) as i:
                    for q in range(QPL):
                        pe.wait_ge(gathered[q], i * (16 * GROUP) + 16 * GROUP * (p * LOOPS + 1))
                        pe.wait_ge(sel_ready, selected(p, i * QPL + q))
                        pe.wait_ge(acc_done, added(p, i * RING + (q - 2) * GROUP + GROUP - 1))
                        for g in range(GROUP):
                            last = pe.matmul(ps[:, q % 2, g * P:(g + 1) * P], ring[:, q * GROUP + g, 0:D], onehot[:, q % 2, g, :], start=True, stop=True)
                        last.then_inc(mm_done, GROUP)

            pe.wait_ge(ld_wA, 16)
            transposed("ln0", 3, lambda c: pe.wait_ge(normed, c + 1))
            rows_of("pre_rows", [(4, A("pre"))], lambda c: await_out(pe, "ln0", c))
            product("pre_T", [(A("pre"), 4)], lambda c: await_out(pe, "ln0", c))
            settled("pre_rows", "pre_T")
            for l in range(LAYERS):
                sum_edges(l)
                product(f"xn{l}", [(A(f"c{l}"), 0)], lambda c: pe.wait_ge(acc_done, added(l, SLOTS - 1)))
                product(f"h{l}", [(A(f"n{l}"), 1), (A(f"s{l}"), 2)], lambda c: await_out(pe, f"xn{l}", c))
                transposed(f"rows{l}", 2, lambda c: await_out(pe, f"h{l}", c))
                settled(f"h{l}", f"rows{l}")

            pe.wait_ge(ld_wB, 16)
            pe.wait_ge(ld_misc, 80)
            transposed("ln1", 3, lambda c: pe.wait_ge(normed, CHUNKS + c + 1))
            product("H", [(B("W1"), 4)], lambda c: await_out(pe, "ln1", c))
            product("G", [(B("WA"), 5)], lambda c: await_out(pe, "H", c))
            for c in range(CHUNKS):
                u = FIRST["t1"] + c
                free_banks(pe, u)
                await_out(pe, "G", c)
                for b in range(CB):
                    pe.transpose(unit(u)[:, b * P:(b + 1) * P], block_of(5, c * CB + b), ident)
                four_more(u, c, 1, side[:, 0, :]).then_inc(node_done, 1)
            settled("t1")
            pe.wait_ge(acc_done, added(3, -1))
            with pe.Fori(0, LOOPS) as i:
                for q in range(QPL):
                    pe.wait_ge(gathered[q], i * (16 * GROUP) + 16 * GROUP * (3 * LOOPS + 1))
                    pe.wait_ge(sel_ready, selected(3, i * QPL + q))
                    for g in range(GROUP):
                        s = q * GROUP + g
                        pe.wait_ge(scaled_ready, i * RING + s + 1)
                        pe.wait_ge(acc_done, added(3, i * RING + s - 4))
                        pe.matmul(ps[0:W_L1 - D, 2 * (s % 4) + 1, 0:P], ring[:, s, D:W_L1], onehot[:, q % 2, g, :], start=True, stop=True)
                        pe.matmul(ps[:, 2 * (s % 4), :], ring[:, s, 0:D], scaled[:, s % 4, :], start=True, stop=True).then_inc(mm_done, 1)
            for c in range(CHUNKS):
                for m in range(MIX):
                    u = FIRST["mix"] + MIX * c + m
                    free_banks(pe, u)
                    pe.wait_ge(sw_ready, c + 1)
                    for a, z in ((0, 512), (512, CH)):
                        last = pe.matmul(unit(u)[:, a:z], pick[0:MIX, m, :], pl[0:MIX, 4, c * CH + a:c * CH + z], start=True, stop=True)
                    last.then_inc(node_done, 1)
            rows_of("o1", [(0, B("o_agg")), (5, B("o_H"))], lambda c: pe.wait_ge(gated, 5 * CHUNKS + c + 1))

            transposed("ln2", 3, lambda c: pe.wait_ge(normed, 2 * CHUNKS + c + 1))
            rows_of("t2", [(2, B("W1s"))], lambda c: await_out(pe, "ln2", c))
            rows_of("hb", [(2, B("W1d"))], lambda c: None)
            settled("t2", "hb")
            pe.wait_ge(c_moved, 48)
            pe.wait_ge(ld_blk, 16)

            def max_step(it, q):
                at = LOOPS if isinstance(it, str) else it
                T = at * QPL + q
                if not isinstance(it, str):
                    pe.wait_ge(gathered[q], at * (16 * GROUP) + 16 * GROUP * (4 * LOOPS + 1))
                    pe.wait_ge(st_ready, T + 1)
                    pe.wait_ge(hid_out, T + (QPL - 1))
                    first = blocks_at(mybir.EngineType.PE, at * RING + q * GROUP)
                    for g in range(GROUP):
                        s = q * GROUP + g
                        to = ps[:, q % 2, g * P:(g + 1) * P]
                        cut = slice(g * P, (g + 1) * P)
                        pe.matmul(to, selT[:, q % 2, cut], pl[:, 5, bass.ds(first[g], P)], start=True, stop=False)
                        pe.matmul(to, ident, ring[:, s, 0:D], start=False, stop=False)
                        last = pe.matmul(to, w9[0:9, q, cut], c9[:, :], start=False, stop=True)
                    last.then_inc(mm_done, GROUP)
                if stages_of(it, q, 1):
                    pe.wait_ge(hid_out, T + QPL)
                    for g in range(GROUP):
                        last = pe.transpose(ps[:, 2, g * P:(g + 1) * P], hid[:, (q - 1) % 2, g, :], ident)
                    last.then_inc(hidT_done, 1)
                if stages_of(it, q, 3):
                    pe.wait_ge(runT_out, T + (QPL - 2))
                    pe.wait_ge(sel_ready, selected(4, T - 3))
                    pe.wait_ge(acc_done, added(4, at * RING + (q - 5) * GROUP + GROUP - 1))
                    for g in range(GROUP):
                        last = pe.matmul(ps[:, 5 + (q - 3) % 2, g * P:(g + 1) * P], runT[:, g, :], onehot[:, (q - 3) % 2, g, :], start=True, stop=True)
                    last.then_inc(maxed, 1)
                if stages_of(it, q, 1):
                    pe.wait_ge(hidT_out, T + QPL)
                    pe.wait_ge(msg_out, T + (QPL - 1))
                    pe.matmul(ps[:, 3, :], B("W2"), hidT, start=True, stop=True).then_inc(msg_done, 1)
                if stages_of(it, q, 2):
                    pe.wait_ge(run_ready, T + (QPL - 1))
                    pe.wait_ge(runT_out, T + (QPL - 2))
                    for g in range(GROUP):
                        last = pe.transpose(ps[:, 4, g * P:(g + 1) * P], run[:, (q - 2) % 2, g * P:(g + 1) * P], ident)
                    last.then_inc(runT_done, 1)

            for q in range(QPL):
                max_step(0, q)
            with pe.Fori(1, LOOPS) as i:
                for q in range(QPL):
                    max_step(i, q)
            for q in range(3):
                max_step("end", q)
            product("u", [(B("U1h"), 2), (B("U1a"), 0)], lambda c: pe.wait_ge(acc_done, added(4, SLOTS - 1)))
            rows_of("o2", [(3, B("U2"))], lambda c: await_out(pe, "u", c))

            pe.wait_ge(ld_wA, 32)
            transposed("ln3", 3, lambda c: pe.wait_ge(normed, 3 * CHUNKS + c + 1))
            rows_of("t3", [(2, A3("msg"))], lambda c: await_out(pe, "ln3", c), (2, side[:, 1, :]))
            product("ad", [(A3("att_d"), 2)], lambda c: None)
            settled("t3", "ad")
            sum_edges(5)
            all_added = lambda c: pe.wait_ge(acc_done, added(5, SLOTS - 1))
            product("r", [(A3("ir"), 0), (A3("hr"), 2)], all_added)
            product("z", [(A3("iz"), 0), (A3("hz"), 2)], all_added)
            product("hn", [(A3("hn"), 2)], all_added)
            product("in", [(A3("in"), 0)], all_added)
            transposed("o3", 4, lambda c: pe.wait_ge(gated, 7 * CHUNKS + c + 1))


def lay_out(inputs):
    import numpy as np
    g = {k: np.asarray(v) for k, v in inputs.items()}
    io = {}
    io["x"] = np.concatenate([g["x"], np.zeros((NP_ - N, D), g["x"].dtype)])
    pad = TPAD * P - E
    i32 = g["dst"].dtype
    dst = np.concatenate([g["dst"], np.full(pad, NP_ - 1, i32)])
    src = np.concatenate([g["src"], np.zeros(pad, i32)])
    far = np.full(1, -1, i32)
    rows = [src, dst, np.concatenate([far, dst[:-1]]), np.concatenate([dst[1:], far])]
    io["edges"] = np.stack([r.reshape(TPAD, P) for r in rows], axis=1)
    io["ends"] = dst.reshape(SJ, P, P)[:, :, [0, P - 1]].transpose(1, 0, 2)
    io["weights"] = np.concatenate([g["edge_weight"], np.zeros(pad, g["edge_weight"].dtype)]).reshape(TPAD, P)
    f = g["x"].dtype
    a = np.arange(P)
    io["cst"] = np.concatenate([
        np.eye(P), np.tile(a, (P, 1)), (a[:, None] < a[None, :]), np.ones((P, P)),
        a[:, None] + P * np.arange(SJ)[None, :], np.tile(np.arange(SPAD), (P, 1))], axis=1).astype(f)
    upd, conv = g["L0_gnn_W_upd"], g["L0_gnn_W_conv"]
    io["matsA0"] = np.stack([g["L0_gnn_W_pre"], *conv, *[u[:D] for u in upd], *[u[D:] for u in upd]], axis=1)
    ih, hh = g["L3_gnn_W_ih"], g["L3_gnn_W_hh"]
    att = g["L3_gnn_W_att"]
    io["matsA3"] = np.stack([g["L3_gnn_W_msg"]] + [m[k * D:(k + 1) * D].T for m in (ih, hh) for k in range(3)]
                            + [np.broadcast_to(att[D:], (D, P))], axis=1)
    w2, w1, u1 = g["L1_gnn_W2"], g["L2_gnn_W1"], g["L2_gnn_U1"]
    io["matsB"] = np.stack([g["L1_gnn_W1"].T, g["L1_gnn_WA"].T, w2[:, :D].T, w2[:, D:].T,
                            w1[:D], w1[D:2 * D], g["L2_gnn_W2"], u1[:D], u1[D:], g["L2_gnn_U2"]], axis=1)
    bi, bh = g["L3_gnn_b_ih"].reshape(3, D), g["L3_gnn_b_hh"].reshape(3, D)
    io["cols"] = np.stack([g["L0_gnn_b_pre"], *g["L0_gnn_b_conv"], *g["L0_gnn_b_upd"], g["L1_gnn_b1"], g["L2_gnn_b2"],
                           g["L2_gnn_c1"], np.broadcast_to(g["L3_gnn_b_att"], (D,)), bi[0], bi[1], bi[2], bh[2], bh[0], bh[1],
                           g["L3_gnn_gamma"], g["L3_gnn_beta"]], axis=1)
    io["brow"] = np.stack([g["L0_gnn_b_pre"], g["L1_gnn_b2"], g["L2_gnn_b1"], g["L2_gnn_c2"], g["L3_gnn_b_msg"]])
    io["side"] = np.stack([g["L1_gnn_WB"].T, np.concatenate([att[:D], np.zeros((D, 3), f)], axis=1)], axis=1)
    io["pick"] = np.tile((np.arange(MIX)[:, None, None] == np.arange(MIX)[None, :, None]).astype(f), (1, 1, P))
    io["w1c"] = np.ascontiguousarray(w1[2 * D:])
    return {k: np.ascontiguousarray(v) for k, v in io.items()}


def kernel(**inputs):
    import numpy as _np
    import concourse.bacc as _bacc
    from concourse import mybir as _mybir
    from concourse.bass_utils import run_bass_kernel_spmd as _run

    nc = _bacc.Bacc("TRN2", target_bir_lowering=False, num_devices=1)
    arrays, io = {}, {}
    for name, a in lay_out(inputs).items():
        arrays[f"in_{name}"] = a
        io[name] = nc.dram_tensor(f"in_{name}", a.shape, _mybir.dt.from_np(a.dtype), kind="ExternalInput").ap()
    out = nc.dram_tensor("out_0", (NP_, D), _mybir.dt.from_np(_np.dtype("float32")), kind="ExternalOutput").ap()
    gnn(nc, io, out)
    r = _run(nc, [arrays], core_ids=[0])
    return r.results[0]["out_0"][:N]
```

```python
import concourse.bass as bass
from concourse import mybir
from contextlib import ExitStack

D = 128
N = 6250
E = 100000
P = 128
BLOCKS = -(-N // P)
NP_ = BLOCKS * P
TILES = -(-E // P)
GROUP = 4
RING = 16
SLOTS = -(-(TILES + BLOCKS - 1) // RING) * RING
SJ = -(-(SLOTS + GROUP) // P)
SPAD = SJ * P
TPAD = SJ * P
QUADS = SLOTS // GROUP
QPL = RING // GROUP
CREDIT = RING + GROUP
LOOPS = SLOTS // RING
CB = 7
CH = CB * P
CHUNKS = BLOCKS // CB
MIX = 4
BY_V = (0, 2)
LAG_O = 2
PARTS = 3
BANK_BLOCKS = 14
LAYERS = 3
ONES = 160
W_L1 = ONES + MIX
W_L3 = D + 4
EPS = 1e-5
FAR = -10000.0
LOW = -3.0e38

MATS_A0 = ["pre", "c0", "c1", "c2", "n0", "n1", "n2", "s0", "s1", "s2"]
MATS_A3 = ["msg", "ir", "iz", "in", "hr", "hz", "hn", "att_d"]
MATS_B = ["W1", "WA", "o_agg", "o_H", "W1s", "W1d", "W2", "U1h", "U1a", "U2"]
COLS = ["pre", "c0", "c1", "c2", "u0", "u1", "u2", "g_b1", "b2", "c1_", "att", "r", "z", "in", "hn", "r2", "z2", "gamma", "beta", "b1_"]
ROWS = ["pre", "o1", "o2", "msg"]

STAGES = [("off", "V", 1), ("slot", "V", 1), ("t_idx", "V", 1), ("t_dl0", "A", 1), ("t_dl", "V", 1), ("t_dlL", "A", 1),
          ("ln0", "A", CHUNKS), ("pre_rows", "V", CHUNKS), ("pre_T", "A", CHUNKS)]
for _l in range(LAYERS):
    STAGES += [(f"xn{_l}", "A", CHUNKS), (f"h{_l}", "A", CHUNKS), (f"rows{_l}", "V", CHUNKS)]
STAGES += [("ln1", "A", CHUNKS), ("H", "A", CHUNKS), ("G", "A", CHUNKS), ("t1", "V", CHUNKS),
           ("sumT", "V", 2), ("meanT", "A", CHUNKS)]
for _c in range(CHUNKS + LAG_O):
    STAGES += [(f"mix{_c}", "V", MIX)] if _c < CHUNKS else []
    STAGES += [(f"o1_{_c - LAG_O}", "V", 1)] if _c >= LAG_O else []
STAGES += [("ln2", "A", CHUNKS), ("t2", "A", CHUNKS), ("hb", "V", CHUNKS), ("u", "A", CHUNKS), ("o2", "V", CHUNKS),
           ("ln3", "A", CHUNKS), ("t3", "V", CHUNKS), ("ad", "A", CHUNKS),
           ("r", "A", CHUNKS), ("z", "A", CHUNKS), ("hn", "A", CHUNKS), ("in", "V", CHUNKS), ("o3", "V", CHUNKS)]
EVAC = [e for _, e, n in STAGES for _ in range(n)]
FIRST = {}
_u = 0
for _name, _, _n in STAGES:
    FIRST[_name] = _u
    _u += _n


def evacs(u):
    return EVAC[:u + 1].count(EVAC[u])


PASSES = ["L0a", "L0b", "L0c", "L1", "L2", "L3"]


def gnn(nc, io, out, debug=None):
    fp32, i32, bf16 = mybir.dt.float32, mybir.dt.int32, mybir.dt.bfloat16
    DVE = mybir.EngineType.DVE
    ALU, ACT = mybir.AluOpType, mybir.ActivationFunctionType

    ctx = ExitStack()
    with ctx:
        def sb(name, shape, dt=fp32):
            return ctx.enter_context(nc.sbuf_tensor(name, shape, dt))

        def sem(name):
            return ctx.enter_context(nc.semaphore(name))

        def dram(name, shape, dt=fp32):
            return nc.dram_tensor(name, shape, dt)

        tab0 = [dram(f"tab_L0_{l}", [NP_, D]) for l in range(LAYERS)]
        tab1 = dram("tab_L1", [NP_, W_L1])
        tab2 = dram("tab_L2", [NP_, D])
        tab3 = dram("tab_L3", [NP_, W_L3])
        x_keep = dram("x_keep", [NP_, D])
        blk_d = dram("blk_d", [SPAD], i32)
        rows_d = dram("rows_d", [2, SPAD, P], bf16)
        w_d = dram("w_d", [9, SPAD, P], bf16)
        c_d = dram("c_d", [3, D], bf16)

        pl = sb("planes", [P, 6, NP_])
        chunk = lambda p, c: pl[:, p, c * CH:(c + 1) * CH]
        block_of = lambda p, b: pl[:, p, b * P:(b + 1) * P]

        ring = sb("ring", [P, RING, W_L1])
        onehot = sb("onehot", [P, 2, GROUP, P])
        scaled = sb("scaled", [P, 4, MIX * P])
        idxT = sb("idxT", [P, SPAD], i32)
        idx_now = sb("idx_now", [P, 2, RING], i32)
        dlT = sb("dlT", [P, SPAD])
        dl0T = sb("dl0T", [P, SPAD])
        dlLT = sb("dlLT", [P, SPAD])
        blk = sb("blk", [1, SPAD], i32)
        cst = sb("cst", [P, 2 * P])
        slot_id = sb("slot_id", [P, SJ])
        matA = sb("matA", [P, len(MATS_A0), D])
        matB = sb("matB", [P, len(MATS_B), D])
        cols = sb("cols", [P, len(COLS)])
        brow = sb("brow", [P, len(ROWS), D])
        pick = sb("pick", [PARTS * MIX, MIX, P])
        c9 = sb("c9", [9, D], bf16)
        bn = sb("bn", [P, 2 * CHUNKS, 6])
        fin = sb("fin", [P, 8])
        side = sb("side", [P, 2, 4])
        st = sb("st", [P, BLOCKS, 6])
        stat = sb("stat", [P, 5, BLOCKS])
        small = sb("small", [P, 10, SJ])
        fl = sb("fl", [P, SJ, 2], i32)
        fli = sb("fli", [P, SJ, 2], i32)
        flf = sb("flf", [P, SJ, 2])
        nt = sb("nt", [P, SJ, 2])
        tsi = sb("tsi", [P, SJ], i32)
        bsi = sb("bsi", [P, SJ], i32)

        ident, iota = cst[:, 0:P], cst[:, P:2 * P]
        A = lambda name: matA[:, MATS_A0.index(name), :]
        A3 = lambda name: matA[:, MATS_A3.index(name), :]
        B = lambda name: matB[:, MATS_B.index(name), :]
        col = lambda name: cols[:, COLS.index(name):COLS.index(name) + 1]
        over_blocks = lambda name, k: brow[:, ROWS.index(name), :].rearrange("p (o d) -> p o d", o=1).broadcast_to([P, k, D])

        ps = ctx.enter_context(nc.psum_tensor("ps", [P, 8, 512], fp32))
        flat = ps[:, :, :].rearrange("p b n -> p (b n)")
        unit = lambda u, n=CH: flat[:, (u % 4) * 1024:(u % 4) * 1024 + n]

        ld_first, ld_cst, ld_x, ld_wA, ld_wB, ld_misc = (sem(f"ld_{n}") for n in ("first", "cst", "x", "wA", "wB", "misc"))
        ld_slots = sem("ld_slots")
        st_slots = sem("st_slots")
        ld_blk = sem("ld_blk")
        tab_written = sem("tab_written")
        x_moved = sem("x_moved")
        maxed = sem("maxed")
        means_ready = sem("means_ready")
        mixed = sem("mixed")
        top = sem("top")
        bn_ready = sem("bn_ready")
        dve_setup = sem("dve_setup")
        node_done = sem("node_done")
        out_A, out_V = sem("out_A"), sem("out_V")
        normed = sem("normed")
        sqrt_in, sqrt_out = sem("sqrt_in"), sem("sqrt_out")
        gathered = [sem(f"gathered{q}") for q in range(QPL)]
        idx_ready = [sem(f"idx_ready{h}") for h in range(2)]
        sel_ready = sem("sel_ready")
        mm_done = sem("mm_done")
        acc_done = sem("acc_done")
        scaled_ready = sem("scaled_ready")
        scaled_by_v = sem("scaled_by_v")
        sig_ready = sem("sig_ready")
        rows_in = [sem(f"rows_in{q}") for q in range(QPL)]
        st_ready = sem("st_ready")
        pre_done = sem("pre_done")
        hid_out = sem("hid_out")
        hb_top, hb_mid, hb_low = sem("hb_top"), sem("hb_mid"), sem("hb_low")
        msg_done = sem("msg_done")
        msg_out = sem("msg_out")
        run_ready = sem("run_ready")
        runT_done = sem("runT_done")
        runT_out = sem("runT_out")
        pooled = sem("pooled")
        elem = sem("elem")
        gated = sem("gated")
        x_back = sem("x_back")
        c_moved = sem("c_moved")
        zeroed = sem("zeroed")
        passed = sem("passed")
        stats_done = sem("stats_done")
        done = sem("done")

        block = ctx.enter_context(nc.Block())

        out_sem = {"A": out_A, "V": out_V}

        def free_banks(pe, u):
            if u >= 4:
                pe.wait_ge(out_sem[EVAC[u - 4]], evacs(u - 4))

        def await_out(eng, name, c):
            u = FIRST[name] + c
            eng.wait_ge(out_sem[EVAC[u]], evacs(u))

        def await_unit(eng, name, c):
            eng.wait_ge(node_done, FIRST[name] + c + 1)

        XP = {"L0": 5, "L1": 5, "L2": 1, "L3": 1}
        rows_view = lambda p, w=D: pl[:, p, :].rearrange("p (b d) -> p b d", d=w)
        dram_rows = lambda t: t[:, :].rearrange("(b p) d -> p b d", p=P)

        iota_s = pl[:, 4, 0:SPAD]
        cmp = pl[:, 0, :].rearrange("p (k s) -> p k s", s=SPAD)
        got = pl[:, 1, 0:SJ * 4 * P].bitcast(i32).rearrange("p (j c e) -> p j c e", j=SJ, c=4)
        got_w = pl[:, 2, 0:SJ * P].rearrange("p (j e) -> p j e", j=SJ)
        gotf = pl[:, 3, 0:SJ * 4 * P].rearrange("p (j c e) -> p j c e", j=SJ, c=4)
        base = 4 * SJ * P
        tmpw = lambda n, k=1: pl[:, n, base:base + k * SJ * P]
        eq = tmpw(1).rearrange("p (j e) -> p j e", j=SJ)
        rr = pl[:, 2, SJ * P:2 * SJ * P].bitcast(bf16).rearrange("p (j c e) -> p j c e", j=SJ, c=2)
        dl0r = pl[:, 2, 3 * SJ * P:4 * SJ * P].rearrange("p (j e) -> p j e", j=SJ)
        dlLr = pl[:, 2, 4 * SJ * P:5 * SJ * P].rearrange("p (j e) -> p j e", j=SJ)
        dlr = pl[:, 2, 5 * SJ * P:6 * SJ * P].rearrange("p (j e) -> p j e", j=SJ)
        wpart = pl[:, 4, SPAD:SPAD + 2 * SJ * P].bitcast(bf16).rearrange("p (k j e) -> p k j e", k=4, j=SJ)
        rest = pl[:, 4, 3 * SPAD:4 * SPAD].rearrange("p (j e) -> p j e", j=SJ)
        upper, ones = (pl[:, 4, 4 * SPAD + k * P:4 * SPAD + (k + 1) * P] for k in range(2))
        cw = pl[0:1, 4, 5 * SPAD:5 * SPAD + 2 * D].rearrange("p (c d) -> p c d", c=2)
        cpart = pl[0:1, 4, 5 * SPAD + 2 * D:5 * SPAD + 4 * D].bitcast(bf16).rearrange("p (c d) -> p c d", c=4)[:, 0:3, :]
        mean = scaled[:, 0, 0:BLOCKS * MIX].rearrange("p (b m) -> p b m", m=MIX)
        mrest = scaled[:, 1, 0:BLOCKS * MIX].rearrange("p (b m) -> p b m", m=MIX)
        mpart = scaled[:, 2, 0:BLOCKS * PARTS * MIX // 2].bitcast(bf16).rearrange("p (b k m) -> p b k m", k=PARTS, m=MIX)
        ident_b = scaled[:, 3, 0:P // 2].bitcast(bf16)
        pick_b = scaled[0:PARTS * MIX, 3, P // 2:P // 2 + MIX * P // 2].bitcast(bf16).rearrange("p (m n) -> p m n", m=MIX)
        meanT = pl[0:PARTS * MIX, 4, 0:NP_ // 2].bitcast(bf16)
        W_S = W_L1 - D
        SM = lambda i: small[:, i, :]
        srcf, dstf, dprevf, dnextf = (gotf[:, :, c, :] for c in range(4))

        half = NP_ // 2
        hb_parts = [pl[:, 5, 0:half].bitcast(bf16), pl[:, 5, half:NP_].bitcast(bf16), pl[:, 3, 0:half].bitcast(bf16)]
        hb_rest = scaled[:, :, :].rearrange("p a n -> p (a n)")[:, 0:2 * CH].rearrange("p (t n) -> p t n", t=2)
        part = lambda plane, start, n, k: pl[:, plane, start + n * 512:start + (n + k) * 512]
        selT = part(3, half, 0, 1).bitcast(bf16).rearrange("p (t n) -> p t n", t=2)
        hidT = part(3, half, 1, 2).rearrange("p (t n) -> p t n", t=2)
        msg = part(3, half, 3, 1)
        run = part(3, half, 4, 2).rearrange("p (t n) -> p t n", t=2)
        runT = part(4, 0, 0, 1).rearrange("p (g n) -> p g n", g=GROUP)
        rowbc = part(4, 0, 1, QPL).bitcast(bf16).rearrange("p (q c n) -> p q c n", q=QPL, c=2)
        w9 = part(4, 0, 1 + QPL, QPL // 2).bitcast(bf16).rearrange("p (q n) -> p q n", q=QPL)
        sig = scaled

        def used(p, s):
            return s + (CREDIT + p * SLOTS + 1)

        def added(p, s):
            return s + (CREDIT + p * (SLOTS + 1) + 2)

        def selected(p, q):
            return q + (p * (QUADS + 1) - (1 if p > 4 else 0) + 1)

        def blocks_at(engine, slot):
            return nc.values_load_multi_w_load_instructions(
                blk[0:1, bass.ds(slot, GROUP)], engines=[engine], min_val=0, max_val=NP_ - P,
                skip_runtime_bounds_check_because="the set-up clamps them")[1]

        def stages_of(it, q, lag):
            if isinstance(it, str):
                return q < lag
            return q >= lag if isinstance(it, int) else True

        @block.sync
        def _(sp):
            sp.dma_start(fl[:, :, :], io["ends"]).then_inc(ld_first, 16)
            sp.dma_start(cst[:, :], io["cst"][:, 0:2 * P]).then_inc(ld_cst, 16)
            sp.dma_start(pl[:, 4, 4 * SPAD:4 * SPAD + 2 * P], io["cst"][:, 2 * P:4 * P]).then_inc(ld_cst, 16)
            sp.dma_start(slot_id[:, :], io["cst"][:, 4 * P:4 * P + SJ]).then_inc(ld_cst, 16)
            sp.dma_start(iota_s, io["cst"][:, 4 * P + SJ:4 * P + SJ + SPAD]).then_inc(ld_cst, 16)
            sp.dma_start(rows_view(5), io["x"].rearrange("(b p) d -> p b d", p=P)).then_inc(ld_x, 16)
            sp.dma_start(matA[:, :, :], io["matsA0"]).then_inc(ld_wA, 16)
            sp.dma_start(cols[:, :], io["cols"]).then_inc(ld_misc, 16)
            sp.dma_start(side[:, :, :], io["side"]).then_inc(ld_misc, 16)
            sp.dma_start(brow[:, :, :], io["brow"].rearrange("(o r) d -> o r d", o=1).broadcast_to([P, len(ROWS), D])).then_inc(ld_misc, 16)
            sp.dma_start(pick[:, :, :], io["pick"]).then_inc(ld_misc, 16)
            sp.dma_start(cw[:, 0, :], io["w1c"]).then_inc(ld_misc, 16)
            sp.dma_start(matB[:, :, :], io["matsB"]).then_inc(ld_wB, 16)
            sp.wait_ge(dve_setup, 14)
            sp.dma_start(blk_d[:].rearrange("(j q) -> q j", q=P), bsi[:, :], allow_slow_non_contiguous=True).then_inc(st_slots, 16)
            sp.wait_ge(st_slots, 16)
            sp.dma_start(blk[0:1, :], blk_d[:].rearrange("(o s) -> o s", o=1)).then_inc(ld_blk, 16)
            sp.wait_ge(dve_setup, 23)
            for c in range(2):
                sp.dma_start(rows_d[c].rearrange("(j q) e -> q j e", q=P), rr[:, :, c, :]).then_inc(st_slots, 16)
            sp.wait_ge(dve_setup, 28)
            for k in range(9):
                sp.dma_start(w_d[k].rearrange("(j q) e -> q j e", q=P), wpart[:, k // 3]).then_inc(st_slots, 16)
            sp.wait_ge(dve_setup, 33)
            sp.dma_start(c_d[:, :].rearrange("(o c) d -> o c d", o=1), cpart[:, :, :]).then_inc(st_slots, 16)
            sp.wait_ge(st_slots, 16 * 13)
            for k in range(3):
                sp.dma_start(c9[3 * k:3 * k + 3, :], c_d[:, :]).then_inc(c_moved, 16)

            def table(stage, t, plane, w=D):
                both = pl[:, plane:plane + 2, :].rearrange("p a n -> p (a n)")
                for c in range(CHUNKS):
                    await_out(sp, stage, c)
                    sp.dma_start(dram_rows(t)[:, c * CB:(c + 1) * CB, :],
                                 both[:, c * CB * w:(c + 1) * CB * w].rearrange("p (b d) -> p b d", d=w)).then_inc(tab_written, 16)

            def stage_idx(p, it, h):
                sp.wait_ge(mm_done, used(p, it * RING - RING - 1))
                sp.dma_start(idx_now[:, h, :], idxT[:, bass.ds(it * RING, RING)]).then_inc(idx_ready[h], 16)

            def stage_all(p):
                with sp.Fori(0, LOOPS // 2) as i:
                    for h in range(2):
                        stage_idx(p, i * 2 + h, h)

            def load_rows(it, q):
                sp.wait_ge(run_ready, it * QPL + q + 1)
                s0 = it * RING + q * GROUP
                sp.dma_start(rowbc[:, q], rows_d[:, bass.ds(s0, GROUP), :].rearrange("(o c) g e -> o c (g e)", o=1).broadcast_to([P, 2, GROUP * P])
                             ).then_inc(rows_in[q], 16)
                sp.dma_start(w9[0:9, q, :], w_d[:, bass.ds(s0, GROUP), :].rearrange("k g e -> k (g e)")).then_inc(rows_in[q], 16)

            await_out(sp, "t_idx", 0)
            table("pre_rows", tab0[0], 3)
            stage_all(0)
            table("rows0", tab0[1], 3)
            stage_all(1)
            table("rows1", tab0[2], 3)
            stage_all(2)
            for c in range(CHUNKS):
                sp.wait_ge(elem, c + 1)
                sp.dma_start(dram_rows(x_keep)[:, c * CB:(c + 1) * CB, :], rows_view(2)[:, c * CB:(c + 1) * CB, :]).then_inc(x_moved, 16)
            table("t1", tab1, 3, W_L1)
            stage_all(3)
            sp.wait_ge(x_moved, 16 * CHUNKS)
            for c in range(CHUNKS):
                sp.wait_ge(pooled, 3 * c + 1)
                if c:
                    sp.wait_ge(x_back, 16 * c)
                sp.dma_start(rows_view(1)[:, c * CB:(c + 1) * CB, :], dram_rows(x_keep)[:, c * CB:(c + 1) * CB, :]).then_inc(x_back, 16)
            sp.dma_start(matA[:, 0:len(MATS_A3), :], io["matsA3"]).then_inc(ld_wA, 16)
            table("t2", tab2, 4)
            sp.wait_ge(tab_written, 16 * CHUNKS * 5)
            stage_idx(4, 0, 0)
            with sp.Fori(0, LOOPS // 2) as i:
                for h in range(2):
                    it = i * 2 + h
                    for q in range(QPL - 1):
                        load_rows(it, q)
                    stage_idx(4, it + 1, 1 - h)
                    load_rows(it, QPL - 1)
            load_rows(LOOPS, 0)
            sp.wait_ge(idx_ready[0], 16 * (5 * LOOPS // 2 + 1))
            table("t3", tab3, 3, W_L3)
            stage_all(5)
            for c in range(CHUNKS):
                await_out(sp, "o3", c)
                sp.dma_start(out.rearrange("(b p) d -> p b d", p=P)[:, c * CB:(c + 1) * CB, :], rows_view(1)[:, c * CB:(c + 1) * CB, :]).then_inc(done, 16)
            sp.wait_ge(done, 16 * CHUNKS)

        @block.gpsimd
        def _(pool):
            pool.wait_ge(dve_setup, 9)
            for j in range(SJ):
                pool.indirect_dma_start(got[:, j, :, :].rearrange("p c e -> p (c e)"), None, io["edges"].rearrange("t c e -> t (c e)"),
                                        bass.IndirectOffsetOnAxis(tsi[:, j:j + 1], 0)).then_inc(ld_slots, 16)
            for j in range(SJ):
                pool.indirect_dma_start(got_w[:, j, :], None, io["weights"],
                                        bass.IndirectOffsetOnAxis(tsi[:, j:j + 1], 0)).then_inc(ld_slots, 16)

            def gather(p, table, width):
                pool.wait_ge(tab_written, 16 * CHUNKS * (p + 1))
                with pool.Fori(0, LOOPS // 2) as i:
                    for h in range(2):
                        pool.wait_ge(idx_ready[h], i * 16 + 16 * (p * (LOOPS // 2) + 1 + (1 if p > 4 and h == 0 else 0)))
                        pool.sem_inc(passed)
                        for q in range(QPL):
                            pool.wait_ge(mm_done, used(p, i * (2 * RING) + (h * RING + q * GROUP + GROUP - 1 - RING)))
                            pool.sem_inc(passed)
                            for g in range(GROUP):
                                s = q * GROUP + g
                                pool.indirect_dma_start(ring[:, s, 0:width], None, table[:, :],
                                                        bass.IndirectOffsetOnAxis(idx_now[:, h, s:s + 1], 0)).then_inc(gathered[q], 16)

            for l in range(LAYERS):
                gather(l, tab0[l], D)
            gather(3, tab1, W_L1)
            for c in range(CHUNKS):
                for n, (a, b, m) in enumerate(((0, 1, 1), (2, 3, 3), (0, 2, None))):
                    if m is None:
                        pool.wait_ge(pooled, 3 * c + 2)
                    else:
                        await_out(pool, f"mix{c}", m)
                    pool.tensor_tensor(chunk(a, c), chunk(a, c), chunk(b, c), ALU.add).then_inc(pooled, 1)
            gather(4, tab2, D)
            gather(5, tab3, W_L3)
            for c in range(CHUNKS):
                pool.wait_ge(gated, c + 1)
                pool.tensor_tensor(chunk(3, c), chunk(2, c), chunk(5, c), ALU.subtract).then_inc(pooled, 1)

        @block.vector
        def _(dve):
            chain = [0]

            def link(ins):
                chain[0] += 1
                ins.then_inc(dve_setup, 1)
                dve.wait_ge(dve_setup, chain[0])

            dve.wait_ge(ld_first, 16)
            link(dve.tensor_scalar(fli[:, :, :], fl[:, :, :], 7, None, ALU.arith_shift_right))
            link(dve.tensor_copy(flf[:, :, :], fli[:, :, :]))
            link(dve.memset(nt[:, :, :], 1.0))
            link(dve.scalar_tensor_tensor(nt[:, :, 1], flf[:, :, 1], 1.0, flf[:, :, 0], ALU.add, ALU.subtract))
            link(dve.tensor_tensor_scan(SM(0), nt[:, :, 0], nt[:, :, 1], 0.0, ALU.mult, ALU.add))
            link(dve.tensor_tensor(SM(1), SM(0), nt[:, :, 1], ALU.subtract))
            await_unit(dve, "off", 0)
            dve.tensor_copy(SM(2), unit(FIRST["off"], SJ)).then_inc(out_V, 1)
            dve.wait_ge(out_V, 1)
            dve.wait_ge(ld_cst, 64)
            for k in range(SJ):
                last = dve.tensor_scalar(cmp[:, k, :], iota_s, small[:, 2, k:k + 1], None, ALU.is_ge)
            link(last)
            await_unit(dve, "slot", 0)
            dve.tensor_copy(small[:, 3:5, :].rearrange("p c j -> p j c"), unit(FIRST["slot"], 2 * SJ).rearrange("p (j c) -> p j c", c=2)).then_inc(out_V, 1)
            dve.wait_ge(out_V, 2)
            link(dve.tensor_scalar(SM(5), SM(3), 1.0, None, ALU.subtract))
            link(dve.tensor_copy(tsi[:, :], SM(5)))
            dve.wait_ge(ld_slots, 32 * SJ)
            link(dve.tensor_copy(gotf, got))
            link(dve.tensor_scalar(bsi[:, :], got[:, :, 1, P - 1], 7, None, ALU.arith_shift_right))
            link(dve.tensor_tensor(SM(6), SM(4), bsi[:, :], ALU.subtract))
            link(dve.scalar_tensor_tensor(SM(7), slot_id[:, :], 1.0, SM(6), ALU.add, ALU.subtract))
            link(dve.tensor_scalar(bsi[:, :], SM(7), float(BLOCKS - 1), float(P), ALU.min, ALU.mult))
            link(dve.tensor_scalar(SM(8), SM(7), float(P), None, ALU.mult))
            first = small[:, 8:9, :].rearrange("p o j -> p j o").broadcast_to([P, SJ, P])
            link(dve.tensor_tensor(dlr, dstf, first, ALU.subtract))
            link(dve.tensor_tensor(eq, srcf, dstf, ALU.is_equal))
            link(dve.scalar_tensor_tensor(dl0r, eq, FAR, dlr, ALU.mult, ALU.add))
            link(dve.tensor_tensor(eq, dstf, dnextf, ALU.is_equal))
            link(dve.scalar_tensor_tensor(dlLr, eq, FAR, dlr, ALU.mult, ALU.add))
            link(dve.tensor_tensor(eq, dstf, dprevf, ALU.not_equal))
            link(dve.tensor_scalar(rr[:, :, 1, :], eq, LOW, None, ALU.mult))
            link(dve.tensor_copy(rr[:, :, 0, :], dlr))
            link(dve.tensor_copy(wpart[:, 0], got_w))
            link(dve.tensor_tensor(rest, got_w, wpart[:, 0], ALU.subtract))
            link(dve.tensor_copy(wpart[:, 1], rest))
            link(dve.tensor_tensor(rest, rest, wpart[:, 1], ALU.subtract))
            link(dve.tensor_copy(wpart[:, 2], rest))
            dve.wait_ge(ld_misc, 80)
            link(dve.tensor_copy(cpart[:, 0, :], cw[:, 0, :]))
            link(dve.tensor_tensor(cw[:, 1, :], cw[:, 0, :], cpart[:, 0, :], ALU.subtract))
            link(dve.tensor_copy(cpart[:, 1, :], cw[:, 1, :]))
            link(dve.tensor_tensor(cw[:, 1, :], cw[:, 1, :], cpart[:, 1, :], ALU.subtract))
            link(dve.tensor_copy(cpart[:, 2, :], cw[:, 1, :]))
            await_unit(dve, "t_idx", 0)
            dve.tensor_copy(idxT[:, :], unit(FIRST["t_idx"], SPAD)).then_inc(out_V, 1)
            await_unit(dve, "t_dl", 0)
            dve.tensor_copy(dlT[:, :], unit(FIRST["t_dl"], SPAD)).then_inc(out_V, 1)

            for s_, n_ in ((mm_done, CREDIT), (acc_done, CREDIT), (run_ready, QPL), (hid_out, QPL),
                           (msg_done, QPL), (msg_out, QPL), (runT_done, QPL), (runT_out, QPL), (maxed, QPL)):
                dve.sem_inc(s_, n_)

            def statistics(xp, c):
                for b in range(c * CB, (c + 1) * CB):
                    last = dve.bn_stats(st[:, b, :], rows_view(xp)[:, b, :])
                last.then_inc(stats_done, 1)

            def normalise(n, xp, yp):
                X, Y = rows_view(xp), rows_view(yp)
                dve.wait_ge(stats_done, CHUNKS * (n + 1))
                link(dve.tensor_tensor(stat[:, 0], st[:, :, 1], st[:, :, 4], ALU.add))
                link(dve.tensor_tensor(stat[:, 1], st[:, :, 1], st[:, :, 4], ALU.subtract))
                link(dve.tensor_tensor(stat[:, 2], st[:, :, 2], st[:, :, 5], ALU.add))
                link(dve.tensor_tensor(stat[:, 1], stat[:, 1], stat[:, 1], ALU.mult))
                link(dve.tensor_scalar(stat[:, 2], stat[:, 2], 1.0 / D, EPS, ALU.mult, ALU.add))
                link(dve.scalar_tensor_tensor(stat[:, 2], stat[:, 1], 0.25, stat[:, 2], ALU.mult, ALU.add))
                dve.tensor_scalar(stat[:, 0], stat[:, 0], 0.5, None, ALU.mult).then_inc(sqrt_in, 1)
                dve.wait_ge(sqrt_out, n + 1)
                link(dve.reciprocal(stat[:, 4], stat[:, 3]))
                for b in range(BLOCKS):
                    last = dve.tensor_scalar(Y[:, b, :], X[:, b, :], stat[:, 0, b:b + 1], stat[:, 4, b:b + 1], ALU.subtract, ALU.mult)
                    if b % CB == CB - 1:
                        last.then_inc(normed, 1)

            def rows_to(stage, plane, bias=None):
                for c in range(CHUNKS):
                    await_unit(dve, stage, c)
                    src = unit(FIRST[stage] + c).rearrange("p (b d) -> p b d", d=D)
                    dst = rows_view(plane)[:, c * CB:(c + 1) * CB, :]
                    if bias is None:
                        dve.tensor_copy(dst, src).then_inc(out_V, 1)
                    else:
                        dve.tensor_tensor(dst, src, over_blocks(bias, CB), ALU.add).then_inc(out_V, 1)

            def wide_rows(stage, plane, w, bias):
                both = pl[:, plane:plane + 2, :].rearrange("p a n -> p (a n)")[:, 0:BLOCKS * w].rearrange("p (b d) -> p b d", d=w)
                if w == W_L1:
                    dve.memset(both[:, :, D + MIX:ONES], 0.0)
                    dve.memset(both[:, :, ONES:w], 1.0)
                for c in range(CHUNKS):
                    await_unit(dve, stage, c)
                    src = unit(FIRST[stage] + c, CH).rearrange("p (b d) -> p b d", d=D)
                    dst = both[:, c * CB:(c + 1) * CB, 0:D]
                    if bias is None:
                        dve.tensor_copy(dst, src)
                    else:
                        dve.tensor_tensor(dst, src, over_blocks(bias, CB), ALU.add)
                    dve.tensor_copy(both[:, c * CB:(c + 1) * CB, D:D + 4],
                                    unit(FIRST[stage] + c, CH + 4 * CB)[:, CH:].rearrange("p (b d) -> p b d", d=4)).then_inc(out_V, 1)

            def add_chunk(stage, k, plane, c, stats=True):
                u = FIRST[stage] + k
                await_unit(dve, stage, k)
                x = rows_view(plane)[:, c * CB:(c + 1) * CB, :]
                dve.tensor_tensor(x, x, unit(u).rearrange("p (b d) -> p b d", d=D), ALU.add).then_inc(out_V, 1)
                if stats:
                    dve.wait_ge(out_V, evacs(u))
                    statistics(plane, c)

            def add_to_x(stage, plane, stats=True):
                for c in range(CHUNKS):
                    add_chunk(stage, c, plane, c, stats)

            def bias_x(src, dst, bias, sem_=None):
                for c in range(CHUNKS):
                    ins = dve.tensor_tensor(rows_view(dst)[:, c * CB:(c + 1) * CB, :], rows_view(src)[:, c * CB:(c + 1) * CB, :],
                                            over_blocks(bias, CB), ALU.add)
                    if sem_ is not None:
                        ins.then_inc(sem_, 1)
                    else:
                        last = ins
                if sem_ is None:
                    link(last)

            def one_hots(dl, t, first_slot):
                a = iota.rearrange("p (o n) -> p o n", o=1).broadcast_to([P, GROUP, P])
                b = dl[:, bass.ds(first_slot, GROUP)].rearrange("p (g o) -> p g o", o=1).broadcast_to([P, GROUP, P])
                return dve.tensor_tensor(onehot[:, t % 2], a, b, ALU.is_equal)

            def add_group(p, it, s, bank, ready):
                first = blocks_at(DVE, it * RING + s)
                ready()
                for g in range(GROUP):
                    dve.wait_ge(acc_done, added(p, it * RING + (s + g - 1)))
                    at = pl[:, 0, bass.ds(first[g], P)]
                    dve.tensor_tensor(at, at, ps[:, bank, g * P:(g + 1) * P], ALU.add).then_inc(acc_done, 1)

            def sum_pass(p, dl):
                if p:
                    dve.wait_ge(sel_ready, selected(p, -1))
                one_hots(dl, 0, 0).then_inc(sel_ready, 1)
                dve.memset(pl[:, 0, :], 0.0).then_inc(acc_done, 1)
                with dve.Fori(0, LOOPS) as i:
                    for q in range(QPL):
                        one_hots(dl, q + 1, i * RING + (q + 1) * GROUP).then_inc(sel_ready, 1)
                        add_group(p, i, q * GROUP, q % 2, lambda: dve.wait_ge(mm_done, used(p, i * RING + (q * GROUP + GROUP - 1))))

            dve.wait_ge(ld_x, 16)
            for c in range(CHUNKS):
                statistics(5, c)
            normalise(0, 5, 3)
            rows_to("pre_rows", 3, "pre")
            dve.wait_ge(ld_blk, 16)
            for l in range(LAYERS):
                sum_pass(l, dl0T)
                if l < LAYERS - 1:
                    rows_to(f"rows{l}", 3)
            add_to_x("rows2", 5)

            normalise(1, 5, 3)
            bias_x(5, 2, "o1", elem)
            dve.memset(pl[:, 0, :], 0.0).then_inc(elem, 1)
            await_unit(dve, "t1", 0)
            wide_rows("t1", 3, W_L1, None)
            dve.wait_ge(x_moved, 16 * CHUNKS)
            dve.memset(pl[:, 2, :], 0.0)
            await_out(dve, "t1", CHUNKS - 1)
            for u in range(4):
                dve.memset(ps[:, 2 * u + 1, 0:P], 0.0)
            dve.wait_ge(sel_ready, selected(3, -1))
            one_hots(dlT, 0, 0).then_inc(sel_ready, 1)
            dve.wait_ge(tab_written, 16 * CHUNKS * 4)
            dve.memset(pl[:, 4, :], 0.0).then_inc(acc_done, 1)
            dve.wait_ge(zeroed, 2)

            def scale_last(it, q, g):
                if g == 0:
                    dve.wait_ge(gathered[q % QPL], (it + q // QPL) * (16 * GROUP) + 16 * GROUP * (3 * LOOPS + 1))
                    dve.wait_ge(sel_ready, selected(3, it * QPL + q))
                s = (q % QPL) * GROUP + g
                dve.tensor_scalar(scaled[:, g, (MIX - 1) * P:MIX * P], onehot[:, q % 2, g, :], ring[:, s, D + MIX - 1:D + MIX], None,
                                  ALU.mult).then_inc(scaled_by_v, 1)

            def mix_step(it, q, more=True):
                one_hots(dlT, q + 1, it * RING + (q + 1) * GROUP).then_inc(sel_ready, 1)
                first = blocks_at(DVE, it * RING + q * GROUP)
                for g in range(GROUP):
                    s = q * GROUP + g
                    dve.wait_ge(mm_done, used(3, it * RING + s))
                    dve.wait_ge(acc_done, added(3, it * RING + s - 1))
                    at = pl[:, 0:MIX + 1, bass.ds(first[g], P)]
                    dve.tensor_tensor(at, at, flat[:, (s % 4) * 1024:(s % 4) * 1024 + (MIX + 1) * P].rearrange("p (m n) -> p m n", n=P),
                                      ALU.add).then_inc(acc_done, 1)
                    if more and g in BY_V:
                        scale_last(it, q + 1, g)

            for g in BY_V:
                scale_last(0, 0, g)
            with dve.Fori(0, LOOPS - 1) as i:
                for q in range(QPL):
                    mix_step(i, q)
            for q in range(QPL):
                mix_step(LOOPS - 1, q, more=q < QPL - 1)
            dve.wait_ge(acc_done, added(3, SLOTS - 1))
            dve.tensor_copy(ident_b, ident)
            dve.tensor_copy(pick_b, pick[:, :, :])
            banks = [(unit(FIRST["sumT"] + k // 2, 1024)[:, 512 * (k % 2):512 * (k % 2) + n * W_S].rearrange("p (b c) -> p b c", c=W_S),
                      slice(k * BANK_BLOCKS, k * BANK_BLOCKS + n))
                     for k, n in enumerate(min(BANK_BLOCKS, BLOCKS - k * BANK_BLOCKS) for k in range(4))]
            await_unit(dve, "sumT", 1)
            for sums, b in banks:
                last = dve.tensor_scalar(stat[:, 3, b], sums[:, :, ONES - D], 1.0, None, ALU.max)
            link(last)
            link(dve.reciprocal(stat[:, 4], stat[:, 3]))
            for k, (sums, b) in enumerate(banks):
                n = b.stop - b.start
                last = dve.tensor_tensor(mean[:, b, :], sums[:, :, 0:MIX],
                                         stat[:, 4, b].rearrange("p (b o) -> p b o", o=1).broadcast_to([P, n, MIX]), ALU.mult)
                if k % 2:
                    last.then_inc(out_V, 1)
            dve.wait_ge(out_V, evacs(FIRST["sumT"] + 1))
            link(dve.tensor_copy(mpart[:, :, 0, :], mean))
            link(dve.tensor_tensor(mrest, mean, mpart[:, :, 0, :], ALU.subtract))
            link(dve.tensor_copy(mpart[:, :, 1, :], mrest))
            link(dve.tensor_tensor(mrest, mrest, mpart[:, :, 1, :], ALU.subtract))
            dve.tensor_copy(mpart[:, :, 2, :], mrest).then_inc(means_ready, 1)
            for c in range(CHUNKS + LAG_O):
                if c < CHUNKS:
                    for m in range(MIX):
                        await_unit(dve, f"mix{c}", m)
                        dve.wait_ge(mixed, MIX * c + m + 1)
                        dve.tensor_tensor(chunk(m, c), chunk(m, c), unit(FIRST[f"mix{c}"] + m), ALU.mult).then_inc(out_V, 1)
                if c >= LAG_O:
                    dve.wait_ge(x_back, 16 * (c - LAG_O + 1))
                    add_chunk(f"o1_{c - LAG_O}", 0, 1, c - LAG_O)

            normalise(2, 1, 3)
            dve.memset(pl[:, 0, :], 0.0).then_inc(acc_done, 1)
            dve.wait_ge(normed, 3 * CHUNKS)
            bias_x(1, 1, "o2")
            for c in range(CHUNKS + 1):
                if c < CHUNKS:
                    u = FIRST["hb"] + c
                    dve.wait_ge(hb_top, c + 1)
                    if c >= 2:
                        dve.wait_ge(hb_low, c - 1)
                    cut = slice(c * CH, (c + 1) * CH)
                    dve.tensor_tensor(hb_rest[:, c % 2, :], unit(u), hb_parts[0][:, cut], ALU.subtract).then_inc(out_V, 1)
                if c >= 1:
                    cut = slice((c - 1) * CH, c * CH)
                    dve.wait_ge(hb_mid, c)
                    dve.tensor_tensor(hb_parts[2][:, cut], hb_rest[:, (c - 1) % 2, :], hb_parts[1][:, cut], ALU.subtract).then_inc(hb_low, 1)

            def transposed_one_hots(it, q):
                dve.wait_ge(mm_done, used(4, it * RING + q * GROUP - 2 * GROUP + GROUP - 1))
                dve.wait_ge(rows_in[q % QPL], (it + (q // QPL)) * 32 + 32)
                dve.tensor_scalar(selT[:, q % 2, :], rowbc[:, q % QPL, 0, :], slot_id[:, 0:1], None, ALU.is_equal).then_inc(st_ready, 1)

            transposed_one_hots(0, 0)

            def max_step(it, q):
                at = LOOPS if isinstance(it, str) else it
                T = at * QPL + q
                if stages_of(it, q, 2):
                    dve.wait_ge(msg_out, T + (QPL - 1))
                    dve.wait_ge(runT_done, T + (QPL - 3))
                    dve.wait_ge(run_ready, T + (QPL - 2))
                    before = LOW if (isinstance(it, int) and q == 2) else run[:, (q - 3) % 2, GROUP * P - 1:GROUP * P]
                    dve.tensor_tensor_scan(run[:, (q - 2) % 2, :], rowbc[:, (q - 2) % QPL, 1, :], msg, before, ALU.add, ALU.max).then_inc(run_ready, 1)
                if not isinstance(it, str):
                    transposed_one_hots(at, q + 1)
                if stages_of(it, q, 2):
                    one_hots(dlLT, q, at * RING + (q - 2) * GROUP).then_inc(sel_ready, 1)
                if stages_of(it, q, 3):
                    add_group(4, at, (q - 3) * GROUP, 5 + (q - 3) % 2, lambda: dve.wait_ge(maxed, T + (QPL - 2)))

            for q in range(QPL):
                max_step(0, q)
            with dve.Fori(1, LOOPS) as i:
                for q in range(QPL):
                    max_step(i, q)
            for q in range(3):
                max_step("end", q)
            add_to_x("o2", 1)

            normalise(3, 1, 3)
            dve.wait_ge(acc_done, added(5, -2))
            dve.memset(pl[:, 0, :], 0.0).then_inc(acc_done, 1)
            dve.tensor_tensor(col("r"), col("r"), col("r2"), ALU.add).then_inc(elem, 1)
            dve.tensor_tensor(col("z"), col("z"), col("z2"), ALU.add).then_inc(elem, 1)
            wide_rows("t3", 3, W_L3, "msg")

            def weighted(it, q):
                dve.wait_ge(sig_ready, it * QPL + q + 1)
                for g in range(GROUP):
                    last = dve.scalar_tensor_tensor(onehot[:, q % 2, g, :], iota, dlT[:, bass.ds(it * RING + q * GROUP + g, 1)],
                                                    sig[:, q % 4, g * P:(g + 1) * P], ALU.is_equal, ALU.mult)
                last.then_inc(sel_ready, 1)

            dve.wait_ge(sel_ready, selected(5, -1))
            weighted(0, 0)
            with dve.Fori(0, LOOPS) as i:
                for q in range(QPL):
                    weighted(i, q + 1)
                    add_group(5, i, q * GROUP, q % 2, lambda: dve.wait_ge(mm_done, used(5, i * RING + (q * GROUP + GROUP - 1))))
            for c in range(CHUNKS):
                await_out(dve, "hn", c)
                link(dve.tensor_tensor(chunk(3, c), chunk(3, c), chunk(5, c), ALU.mult))
                await_unit(dve, "in", c)
                dve.tensor_tensor(chunk(5, c), chunk(3, c), unit(FIRST["in"] + c), ALU.add).then_inc(out_V, 1)
            for c in range(CHUNKS):
                dve.wait_ge(pooled, 3 * CHUNKS + c + 1)
                link(dve.tensor_tensor(chunk(3, c), chunk(3, c), chunk(4, c), ALU.mult))
                link(dve.tensor_tensor(chunk(3, c), chunk(3, c), chunk(5, c), ALU.add))
                n = min(CH, N - c * CH) // 2
                for k in range(2):
                    last = dve.bn_stats(bn[:, 2 * c + k, :], chunk(3, c)[:, k * n:(k + 1) * n])
            link(last)
            link(dve.bn_aggr(fin[:, 0:2], bn[:, :, :].rearrange("p a b -> p (a b)")))
            dve.tensor_scalar(fin[:, 2:3], fin[:, 1:2], EPS, None, ALU.add).then_inc(sqrt_in, 1)
            dve.wait_ge(sqrt_out, 5)
            link(dve.reciprocal(fin[:, 4:5], fin[:, 3:4]))
            link(dve.tensor_tensor(fin[:, 5:6], fin[:, 4:5], col("gamma"), ALU.mult))
            link(dve.tensor_tensor(fin[:, 6:7], fin[:, 0:1], fin[:, 5:6], ALU.mult))
            dve.tensor_tensor(fin[:, 7:8], col("beta"), fin[:, 6:7], ALU.subtract).then_inc(bn_ready, 1)
            add_to_x("o3", 1, stats=False)

        @block.scalar
        def _(act):
            act.wait_ge(ld_misc, 80)

            def from_psum(stage, dst, func, bias=None, rows=P):
                for c in range(CHUNKS):
                    await_unit(act, stage, c)
                    if bias is None:
                        act.activation(dst(c), unit(FIRST[stage] + c)[0:rows], func).then_inc(out_A, 1)
                    else:
                        act.activation(dst(c), unit(FIRST[stage] + c), func, bias=col(bias)).then_inc(out_A, 1)

            await_unit(act, "t_dl0", 0)
            act.activation(dl0T[:, :], unit(FIRST["t_dl0"], SPAD), ACT.Copy).then_inc(out_A, 1)
            await_unit(act, "t_dlL", 0)
            act.activation(dlLT[:, :], unit(FIRST["t_dlL"], SPAD), ACT.Copy).then_inc(out_A, 1)

            def root(n):
                act.wait_ge(sqrt_in, n + 1)
                act.activation(stat[:, 3], stat[:, 2], ACT.Sqrt).then_inc(sqrt_out, 1)

            root(0)
            act.wait_ge(st_slots, 16 * 13)
            from_psum("ln0", lambda c: chunk(4, c), ACT.Relu)
            from_psum("pre_T", lambda c: chunk(2, c), ACT.Identity, "pre")
            for l in range(LAYERS):
                from_psum(f"xn{l}", lambda c: chunk(1, c), ACT.Identity, f"c{l}")
                from_psum(f"h{l}", lambda c: chunk(2, c), ACT.Relu, f"u{l}")

            root(1)
            from_psum("ln1", lambda c: chunk(4, c), ACT.Relu)
            act.wait_ge(elem, CHUNKS)
            from_psum("H", lambda c: chunk(5, c), ACT.Gelu, "g_b1")
            from_psum("G", lambda c: chunk(1, c), ACT.Gelu)
            act.wait_ge(elem, CHUNKS + 1)
            await_unit(act, "t1", CHUNKS - 1)
            act.activation(pl[:, 1, :], pl[:, 0, :], ACT.Copy).then_inc(zeroed, 1)
            act.wait_ge(tab_written, 16 * CHUNKS * 4)
            act.activation(pl[:, 3, :], pl[:, 0, :], ACT.Copy).then_inc(zeroed, 1)
            with act.Fori(0, LOOPS) as i:
                for q in range(QPL):
                    act.wait_ge(gathered[q], i * (16 * GROUP) + 16 * GROUP * (3 * LOOPS + 1))
                    act.wait_ge(sel_ready, selected(3, i * QPL + q))
                    for g in range(GROUP):
                        s = q * GROUP + g
                        act.wait_ge(mm_done, used(3, i * RING + s - 4))
                        for m in range(MIX - 1 if g in BY_V else MIX):
                            last = act.activation(scaled[:, s % 4, m * P:(m + 1) * P], onehot[:, q % 2, g, :], ACT.Copy,
                                                  scale=ring[:, s, D + m:D + m + 1])
                        last.then_inc(scaled_ready, 1)
            act.wait_ge(acc_done, added(3, SLOTS - 1))
            for c in range(CHUNKS + 2):
                if c < CHUNKS:
                    for m in range(MIX):
                        act.activation(chunk(m, c), chunk(m, c), ACT.Gelu).then_inc(mixed, 1)
                    if c == 0:
                        from_psum("meanT", lambda c: meanT[:, c * CH:(c + 1) * CH], ACT.Copy, rows=PARTS * MIX)
                if 1 <= c <= CHUNKS:
                    act.activation(chunk(5, c - 1), chunk(5, c - 1), ACT.Gelu).then_inc(top, 1)
                if c >= 2:
                    act.wait_ge(pooled, 3 * (c - 1))
                    act.activation(chunk(0, c - 2), chunk(0, c - 2), ACT.Gelu).then_inc(top, 1)

            root(2)
            from_psum("ln2", lambda c: chunk(2, c), ACT.Relu)
            from_psum("t2", lambda c: chunk(4, c), ACT.Copy)
            for c in range(CHUNKS + 1):
                if c < CHUNKS:
                    await_unit(act, "hb", c)
                    act.activation(hb_parts[0][:, c * CH:(c + 1) * CH], unit(FIRST["hb"] + c), ACT.Copy).then_inc(hb_top, 1)
                if c >= 1:
                    await_out(act, "hb", c - 1)
                    act.activation(hb_parts[1][:, (c - 1) * CH:c * CH], hb_rest[:, (c - 1) % 2, :], ACT.Copy).then_inc(hb_mid, 1)

            def max_step(it, q):
                at = LOOPS if isinstance(it, str) else it
                T = at * QPL + q
                if not isinstance(it, str):
                    act.wait_ge(mm_done, used(4, at * RING + q * GROUP + GROUP - 1))
                    act.wait_ge(msg_done, T + (QPL - 1))
                    act.activation(hidT[:, q % 2, :], ps[:, q % 2, :], ACT.Relu, bias=col("b1_")).then_inc(hid_out, 1)
                if stages_of(it, q, 1):
                    act.wait_ge(msg_done, T + QPL)
                    act.wait_ge(run_ready, T + (QPL - 1))
                    act.activation(msg, ps[:, 3, :], ACT.Identity, bias=col("b2")).then_inc(msg_out, 1)
                if stages_of(it, q, 2):
                    act.wait_ge(runT_done, T + (QPL - 1))
                    act.wait_ge(maxed, T + (QPL - 2))
                    act.activation(runT[:, :, :], ps[:, 4, :].rearrange("p (g n) -> p g n", g=GROUP), ACT.Copy).then_inc(runT_out, 1)

            for q in range(QPL):
                max_step(0, q)
            with act.Fori(1, LOOPS) as i:
                for q in range(QPL):
                    max_step(i, q)
            for q in range(3):
                max_step("end", q)
            from_psum("u", lambda c: chunk(3, c), ACT.Relu, "c1_")

            root(3)
            from_psum("ln3", lambda c: chunk(2, c), ACT.Relu)
            from_psum("ad", lambda c: chunk(5, c), ACT.Identity, "att")
            act.wait_ge(ld_blk, 16)

            def attention(it, q):
                act.wait_ge(gathered[q % QPL], (it + q // QPL) * (16 * GROUP) + 16 * GROUP * (5 * LOOPS + 1))
                act.wait_ge(sel_ready, selected(5, it * QPL + q - 4))
                first = blocks_at(mybir.EngineType.Activation, it * RING + q * GROUP)
                for g in range(GROUP):
                    s = q * GROUP + g
                    last = act.activation(sig[:, q % 4, g * P:(g + 1) * P], pl[:, 5, bass.ds(first[g], P)], ACT.Sigmoid,
                                          bias=ring[:, s % RING, D:D + 1])
                last.then_inc(sig_ready, 1)

            with act.Fori(0, LOOPS) as i:
                for q in range(QPL):
                    attention(i, q)
            act.wait_ge(sel_ready, selected(5, QUADS - 4))
            act.activation(sig[:, 0, :], pl[:, 5, 0:512], ACT.Copy).then_inc(sig_ready, 1)
            act.wait_ge(elem, CHUNKS + 3)
            from_psum("r", lambda c: chunk(3, c), ACT.Sigmoid, "r")
            from_psum("z", lambda c: chunk(4, c), ACT.Sigmoid, "z")
            from_psum("hn", lambda c: chunk(5, c), ACT.Identity, "hn")
            for c in range(CHUNKS):
                await_out(act, "in", c)
                act.activation(chunk(5, c), chunk(5, c), ACT.Tanh, bias=col("in")).then_inc(gated, 1)
            act.wait_ge(sqrt_in, 5)
            act.activation(fin[:, 3:4], fin[:, 2:3], ACT.Sqrt).then_inc(sqrt_out, 1)
            act.wait_ge(bn_ready, 1)
            for c in range(CHUNKS):
                act.activation(chunk(4, c), chunk(3, c), ACT.Identity, scale=fin[:, 5:6], bias=fin[:, 7:8]).then_inc(gated, 1)

        @block.tensor
        def _(pe):
            pe.wait_ge(ld_cst, 64)
            pe.wait_ge(dve_setup, 6)
            u = FIRST["off"]
            pe.matmul(unit(u, SJ), upper, nt[:, :, 1], start=True, stop=False)
            pe.matmul(unit(u, SJ), ones, SM(1), start=False, stop=True).then_inc(node_done, 1)
            pe.wait_ge(dve_setup, 7)
            u = FIRST["slot"]
            for j in range(SJ):
                for k in range(SJ):
                    last = pe.matmul(unit(u, 2 * SJ)[:, 2 * j:2 * j + 2], cmp[:, k, j * P:(j + 1) * P], nt[:, k, :],
                                     start=(k == 0), stop=(k == SJ - 1))
            last.then_inc(node_done, 1)
            for name, src, after in (("t_idx", srcf, 10), ("t_dl0", dl0r, 18), ("t_dl", dlr, 20), ("t_dlL", dlLr, 20)):
                pe.wait_ge(dve_setup, after)
                u = FIRST[name]
                free_banks(pe, u)
                for j in range(SJ):
                    last = pe.transpose(unit(u, SPAD)[:, j * P:(j + 1) * P], src[:, j, :], ident)
                last.then_inc(node_done, 1)

            def transposed(stage, plane, ready):
                for c in range(CHUNKS):
                    u = FIRST[stage] + c
                    free_banks(pe, u)
                    ready(c)
                    for b in range(CB):
                        last = pe.transpose(unit(u)[:, b * P:(b + 1) * P], block_of(plane, c * CB + b), ident)
                    last.then_inc(node_done, 1)

            def rows_of(stage, terms, ready, extra=None):
                for c in range(CHUNKS):
                    rows_chunk(stage, c, c, terms, lambda: ready(c), extra)

            def rows_chunk(stage, k, c, terms, ready, extra=None):
                u = FIRST[stage] + k
                free_banks(pe, u)
                ready()
                for b in range(CB):
                    for n, (plane, mat) in enumerate(terms):
                        last = pe.matmul(unit(u)[:, b * P:(b + 1) * P], block_of(plane, c * CB + b), mat,
                                         start=(n == 0), stop=(n == len(terms) - 1))
                if extra:
                    last = four_more(u, c, *extra)
                last.then_inc(node_done, 1)

            def four_more(u, c, plane, mat):
                for b in range(CB):
                    last = pe.matmul(unit(u, 1024)[:, CH + 4 * b:CH + 4 * b + 4], block_of(plane, c * CB + b), mat, start=True, stop=True)
                return last

            def product(stage, terms, ready):
                for c in range(CHUNKS):
                    u = FIRST[stage] + c
                    free_banks(pe, u)
                    ready(c)
                    for a, z in ((0, 512), (512, CH)):
                        for n, (mat, plane) in enumerate(terms):
                            last = pe.matmul(unit(u)[:, a:z], mat, chunk(plane, c)[:, a:z], start=(n == 0), stop=(n == len(terms) - 1))
                    last.then_inc(node_done, 1)

            def settled(*stages):
                for stage in stages:
                    await_out(pe, stage, CHUNKS - 1)

            def sum_edges(p):
                with pe.Fori(0, LOOPS) as i:
                    for q in range(QPL):
                        pe.wait_ge(gathered[q], i * (16 * GROUP) + 16 * GROUP * (p * LOOPS + 1))
                        pe.wait_ge(sel_ready, selected(p, i * QPL + q))
                        pe.wait_ge(acc_done, added(p, i * RING + (q - 2) * GROUP + GROUP - 1))
                        for g in range(GROUP):
                            last = pe.matmul(ps[:, q % 2, g * P:(g + 1) * P], ring[:, q * GROUP + g, 0:D], onehot[:, q % 2, g, :], start=True, stop=True)
                        last.then_inc(mm_done, GROUP)

            pe.wait_ge(ld_wA, 16)
            transposed("ln0", 3, lambda c: pe.wait_ge(normed, c + 1))
            rows_of("pre_rows", [(4, A("pre"))], lambda c: await_out(pe, "ln0", c))
            product("pre_T", [(A("pre"), 4)], lambda c: await_out(pe, "ln0", c))
            settled("pre_rows", "pre_T")
            for l in range(LAYERS):
                sum_edges(l)
                product(f"xn{l}", [(A(f"c{l}"), 0)], lambda c: pe.wait_ge(acc_done, added(l, SLOTS - 1)))
                product(f"h{l}", [(A(f"n{l}"), 1), (A(f"s{l}"), 2)], lambda c: await_out(pe, f"xn{l}", c))
                transposed(f"rows{l}", 2, lambda c: await_out(pe, f"h{l}", c))
                settled(f"h{l}", f"rows{l}")

            pe.wait_ge(ld_wB, 16)
            pe.wait_ge(ld_misc, 80)
            transposed("ln1", 3, lambda c: pe.wait_ge(normed, CHUNKS + c + 1))
            product("H", [(B("W1"), 4)], lambda c: await_out(pe, "ln1", c))
            product("G", [(B("WA"), 5)], lambda c: await_out(pe, "H", c))
            for c in range(CHUNKS):
                u = FIRST["t1"] + c
                free_banks(pe, u)
                await_out(pe, "G", c)
                for b in range(CB):
                    pe.transpose(unit(u)[:, b * P:(b + 1) * P], block_of(5, c * CB + b), ident)
                four_more(u, c, 1, side[:, 0, :]).then_inc(node_done, 1)
            settled("t1")
            pe.wait_ge(acc_done, added(3, -1))
            with pe.Fori(0, LOOPS) as i:
                for q in range(QPL):
                    pe.wait_ge(gathered[q], i * (16 * GROUP) + 16 * GROUP * (3 * LOOPS + 1))
                    pe.wait_ge(sel_ready, selected(3, i * QPL + q))
                    for g in range(GROUP):
                        s = q * GROUP + g
                        pe.wait_ge(scaled_ready, i * RING + s + 1)
                        if g in BY_V:
                            pe.wait_ge(scaled_by_v, i * (QPL * len(BY_V)) + q * len(BY_V) + BY_V.index(g) + 1)
                        pe.wait_ge(acc_done, added(3, i * RING + s - 4))
                        pe.matmul(ps[0:W_L1 - D, 2 * (s % 4) + 1, 0:P], ring[:, s, D:W_L1], onehot[:, q % 2, g, :], start=True, stop=True)
                        pe.matmul(ps[:, 2 * (s % 4), :], ring[:, s, 0:D], scaled[:, s % 4, :], start=True, stop=True).then_inc(mm_done, 1)
            pe.wait_ge(acc_done, added(3, SLOTS - 1))
            for k in range(2):
                u = FIRST["sumT"] + k
                free_banks(pe, u)
                for b in range(2 * BANK_BLOCKS * k, min(2 * BANK_BLOCKS * (k + 1), BLOCKS)):
                    at = 512 * (b // BANK_BLOCKS % 2) + b % BANK_BLOCKS * W_S
                    last = pe.transpose(unit(u, 1024)[:, at:at + W_S], pl[0:W_S, 4, b * P:(b + 1) * P], ident[0:W_S, 0:W_S])
                last.then_inc(node_done, 1)
            pe.wait_ge(means_ready, 1)
            for c in range(CHUNKS):
                u = FIRST["meanT"] + c
                free_banks(pe, u)
                for b in range(CB):
                    last = pe.matmul(unit(u)[0:PARTS * MIX, b * P:(b + 1) * P], mpart[:, c * CB + b, :, :].rearrange("p k m -> p (k m)"),
                                     ident_b, start=True, stop=True)
                last.then_inc(node_done, 1)
            for c in range(CHUNKS + LAG_O):
                if c < CHUNKS:
                    await_out(pe, "meanT", c)
                    for m in range(MIX):
                        u = FIRST[f"mix{c}"] + m
                        free_banks(pe, u)
                        for a, z in ((0, 512), (512, CH)):
                            last = pe.matmul(unit(u)[:, a:z], pick_b[:, m, :], meanT[:, c * CH + a:c * CH + z], start=True, stop=True)
                        last.then_inc(node_done, 1)
                if c >= LAG_O:
                    k = c - LAG_O
                    rows_chunk(f"o1_{k}", 0, k, [(0, B("o_agg")), (5, B("o_H"))], lambda: pe.wait_ge(top, min(2 * k + 3, 2 * CHUNKS)))

            transposed("ln2", 3, lambda c: pe.wait_ge(normed, 2 * CHUNKS + c + 1))
            rows_of("t2", [(2, B("W1s"))], lambda c: await_out(pe, "ln2", c))
            rows_of("hb", [(2, B("W1d"))], lambda c: None)
            settled("t2", "hb")
            pe.wait_ge(c_moved, 48)
            pe.wait_ge(hb_low, CHUNKS)
            pe.wait_ge(ld_blk, 16)

            def max_step(it, q):
                at = LOOPS if isinstance(it, str) else it
                T = at * QPL + q
                if not isinstance(it, str):
                    first = blocks_at(mybir.EngineType.PE, at * RING + q * GROUP)
                    pe.wait_ge(gathered[q], at * (16 * GROUP) + 16 * GROUP * (4 * LOOPS + 1))
                    pe.wait_ge(st_ready, T + 1)
                    pe.wait_ge(hid_out, T + (QPL - 1))
                    for g in range(GROUP):
                        s = q * GROUP + g
                        to = ps[:, q % 2, g * P:(g + 1) * P]
                        cut = slice(g * P, (g + 1) * P)
                        pe.matmul(to, ring[:, s, 0:D], ident, start=True, stop=False)
                        for k in range(PARTS):
                            pe.matmul(to, hb_parts[k][:, bass.ds(first[g], P)], selT[:, q % 2, cut], start=False, stop=False)
                        last = pe.matmul(to, c9[:, :], w9[0:9, q, cut], start=False, stop=True)
                    last.then_inc(mm_done, GROUP)
                if stages_of(it, q, 1):
                    pe.wait_ge(hid_out, T + QPL)
                    pe.wait_ge(msg_out, T + (QPL - 1))
                    pe.matmul(ps[:, 3, :], B("W2"), hidT[:, (q - 1) % 2, :], start=True, stop=True).then_inc(msg_done, 1)
                if stages_of(it, q, 3):
                    pe.wait_ge(runT_out, T + (QPL - 2))
                    pe.wait_ge(sel_ready, selected(4, T - 3))
                    pe.wait_ge(acc_done, added(4, at * RING + (q - 5) * GROUP + GROUP - 1))
                    for g in range(GROUP):
                        last = pe.matmul(ps[:, 5 + (q - 3) % 2, g * P:(g + 1) * P], runT[:, g, :], onehot[:, (q - 3) % 2, g, :], start=True, stop=True)
                    last.then_inc(maxed, 1)
                if stages_of(it, q, 2):
                    pe.wait_ge(run_ready, T + (QPL - 1))
                    pe.wait_ge(runT_out, T + (QPL - 2))
                    for g in range(GROUP):
                        last = pe.transpose(ps[:, 4, g * P:(g + 1) * P], run[:, (q - 2) % 2, g * P:(g + 1) * P], ident)
                    last.then_inc(runT_done, 1)

            for q in range(QPL):
                max_step(0, q)
            with pe.Fori(1, LOOPS) as i:
                for q in range(QPL):
                    max_step(i, q)
            for q in range(3):
                max_step("end", q)
            product("u", [(B("U1h"), 2), (B("U1a"), 0)], lambda c: pe.wait_ge(acc_done, added(4, SLOTS - 1)))
            rows_of("o2", [(3, B("U2"))], lambda c: await_out(pe, "u", c))

            pe.wait_ge(ld_wA, 32)
            transposed("ln3", 3, lambda c: pe.wait_ge(normed, 3 * CHUNKS + c + 1))
            rows_of("t3", [(2, A3("msg"))], lambda c: await_out(pe, "ln3", c), (2, side[:, 1, :]))
            product("ad", [(A3("att_d"), 2)], lambda c: None)
            settled("t3", "ad")
            sum_edges(5)
            all_added = lambda c: pe.wait_ge(acc_done, added(5, SLOTS - 1))
            product("r", [(A3("ir"), 0), (A3("hr"), 2)], all_added)
            product("z", [(A3("iz"), 0), (A3("hz"), 2)], all_added)
            product("hn", [(A3("hn"), 2)], all_added)
            product("in", [(A3("in"), 0)], all_added)
            transposed("o3", 4, lambda c: pe.wait_ge(gated, CHUNKS + c + 1))


def lay_out(inputs):
    import numpy as np
    g = {k: np.asarray(v) for k, v in inputs.items()}
    io = {}
    io["x"] = np.concatenate([g["x"], np.zeros((NP_ - N, D), g["x"].dtype)])
    pad = TPAD * P - E
    i32 = g["dst"].dtype
    dst = np.concatenate([g["dst"], np.full(pad, NP_ - 1, i32)])
    src = np.concatenate([g["src"], np.zeros(pad, i32)])
    far = np.full(1, -1, i32)
    rows = [src, dst, np.concatenate([far, dst[:-1]]), np.concatenate([dst[1:], far])]
    io["edges"] = np.stack([r.reshape(TPAD, P) for r in rows], axis=1)
    io["ends"] = dst.reshape(SJ, P, P)[:, :, [0, P - 1]].transpose(1, 0, 2)
    io["weights"] = np.concatenate([g["edge_weight"], np.zeros(pad, g["edge_weight"].dtype)]).reshape(TPAD, P)
    f = g["x"].dtype
    a = np.arange(P)
    io["cst"] = np.concatenate([
        np.eye(P), np.tile(a, (P, 1)), (a[:, None] < a[None, :]), np.ones((P, P)),
        a[:, None] + P * np.arange(SJ)[None, :], np.tile(np.arange(SPAD), (P, 1))], axis=1).astype(f)
    upd, conv = g["L0_gnn_W_upd"], g["L0_gnn_W_conv"]
    io["matsA0"] = np.stack([g["L0_gnn_W_pre"], *conv, *[u[:D] for u in upd], *[u[D:] for u in upd]], axis=1)
    ih, hh = g["L3_gnn_W_ih"], g["L3_gnn_W_hh"]
    att = g["L3_gnn_W_att"]
    io["matsA3"] = np.stack([g["L3_gnn_W_msg"]] + [m[k * D:(k + 1) * D].T for m in (ih, hh) for k in range(3)]
                            + [np.broadcast_to(att[D:], (D, P))], axis=1)
    w2, w1, u1 = g["L1_gnn_W2"], g["L2_gnn_W1"], g["L2_gnn_U1"]
    io["matsB"] = np.stack([g["L1_gnn_W1"].T, g["L1_gnn_WA"].T, w2[:, :D].T, w2[:, D:].T,
                            w1[:D], w1[D:2 * D], g["L2_gnn_W2"], u1[:D], u1[D:], g["L2_gnn_U2"]], axis=1)
    bi, bh = g["L3_gnn_b_ih"].reshape(3, D), g["L3_gnn_b_hh"].reshape(3, D)
    io["cols"] = np.stack([g["L0_gnn_b_pre"], *g["L0_gnn_b_conv"], *g["L0_gnn_b_upd"], g["L1_gnn_b1"], g["L2_gnn_b2"],
                           g["L2_gnn_c1"], np.broadcast_to(g["L3_gnn_b_att"], (D,)), bi[0], bi[1], bi[2], bh[2], bh[0], bh[1],
                           g["L3_gnn_gamma"], g["L3_gnn_beta"], g["L2_gnn_b1"]], axis=1)
    io["brow"] = np.stack([g["L0_gnn_b_pre"], g["L1_gnn_b2"], g["L2_gnn_c2"], g["L3_gnn_b_msg"]])
    io["side"] = np.stack([g["L1_gnn_WB"].T, np.concatenate([att[:D], np.zeros((D, 3), f)], axis=1)], axis=1)
    io["pick"] = np.tile((np.arange(PARTS * MIX)[:, None, None] % MIX == np.arange(MIX)[None, :, None]).astype(f), (1, 1, P))
    io["w1c"] = np.ascontiguousarray(w1[2 * D:])
    return {k: np.ascontiguousarray(v) for k, v in io.items()}


def kernel(**inputs):
    import numpy as _np
    import concourse.bacc as _bacc
    from concourse import mybir as _mybir
    from concourse.bass_utils import run_bass_kernel_spmd as _run

    nc = _bacc.Bacc("TRN2", target_bir_lowering=False, num_devices=1)
    arrays, io = {}, {}
    for name, a in lay_out(inputs).items():
        arrays[f"in_{name}"] = a
        io[name] = nc.dram_tensor(f"in_{name}", a.shape, _mybir.dt.from_np(a.dtype), kind="ExternalInput").ap()
    out = nc.dram_tensor("out_0", (NP_, D), _mybir.dt.from_np(_np.dtype("float32")), kind="ExternalOutput").ap()
    gnn(nc, io, out)
    r = _run(nc, [arrays], core_ids=[0])
    return r.results[0]["out_0"][:N]
```
